# Optimizing a Trainium2 kernel written in Bass

```python
import numpy as np
import jax
import jax.numpy as jnp

def _softmax(x, axis=-1):
    return jax.nn.softmax(x, axis=axis)

def _gelu(x):
    return jax.nn.gelu(x, approximate=True)

def _silu(x):
    return jax.nn.silu(x)

def _sigmoid(x):
    return jax.nn.sigmoid(x)

def _layernorm(x, axis=-1, eps=1e-05):
    m = jnp.mean(x, axis=axis, keepdims=True)
    v = jnp.var(x, axis=axis, keepdims=True)
    return (x - m) / jnp.sqrt(v + eps)

def _scatter_add(tgt, idx, src, axis=0):
    return tgt.at[idx].add(src)

def _segment_sum(src, seg, n):
    return jax.ops.segment_sum(src, seg, n)
kernel_name = 'mk_adaln_d1_jaxref_r8_d9799a'

def setup_inputs(seed: int=0):
    np.random.seed(seed)
    _w = jnp.asarray

    def _L0_attn_setup():
        import math
        import jax, jax.numpy as jnp
        import numpy as np
        N_HEADS = 16
        D_KV = 64
        NUM_BUCKETS = 32
        MAX_DISTANCE = 128

        def _relative_position_bucket(relative_position, num_buckets=NUM_BUCKETS, max_distance=MAX_DISTANCE):
            num_buckets //= 2
            n = -relative_position
            ret = (n < 0).astype(jnp.int32) * num_buckets
            n = jnp.abs(n)
            max_exact = num_buckets // 2
            is_small = n < max_exact
            val_if_large = max_exact + (jnp.log(jnp.maximum(n, 1).astype(jnp.float32) / max_exact) / math.log(max_distance / max_exact) * (num_buckets - max_exact)).astype(jnp.int32)
            val_if_large = jnp.minimum(val_if_large, num_buckets - 1)
            return ret + jnp.where(is_small, n, val_if_large)
        key = jax.random.key(seed)
        ks = jax.random.split(key, 6)
        B, S, D = (2, 256, 128)
        scale = 0.02
        return {'x': jax.random.normal(ks[0], (B, S, D), dtype=jnp.float32), 'Wq': jax.random.normal(ks[1], (D, N_HEADS * D_KV), dtype=jnp.float32) * scale, 'Wk': jax.random.normal(ks[2], (D, N_HEADS * D_KV), dtype=jnp.float32) * scale, 'Wv': jax.random.normal(ks[3], (D, N_HEADS * D_KV), dtype=jnp.float32) * scale, 'Wo': jax.random.normal(ks[4], (N_HEADS * D_KV, D), dtype=jnp.float32) * scale, 'rel_emb': jax.random.normal(ks[5], (NUM_BUCKETS, N_HEADS), dtype=jnp.float32) * scale}
    _L0_attn_in = _L0_attn_setup()

    def _L0_ffn_setup():
        import jax, jax.numpy as jnp
        import numpy as np
        D_MODEL = 128
        HIDDEN = 512
        N_ROUTING = 2
        key = jax.random.key(seed)
        ks = jax.random.split(key, 10)
        s = 0.02
        x = jax.random.normal(ks[0], (4, 512, D_MODEL), dtype=jnp.float32)
        gate_w = jax.random.normal(ks[1], (N_ROUTING, D_MODEL), dtype=jnp.float32) * s
        w1 = jax.random.normal(ks[2], (N_ROUTING, D_MODEL, HIDDEN), dtype=jnp.float32) * s
        b1 = jax.random.normal(ks[3], (N_ROUTING, HIDDEN), dtype=jnp.float32) * s
        w2 = jax.random.normal(ks[4], (N_ROUTING, HIDDEN, D_MODEL), dtype=jnp.float32) * s
        b2 = jax.random.normal(ks[5], (N_ROUTING, D_MODEL), dtype=jnp.float32) * s
        sw1 = jax.random.normal(ks[6], (D_MODEL, HIDDEN), dtype=jnp.float32) * s
        sb1 = jax.random.normal(ks[7], (HIDDEN,), dtype=jnp.float32) * s
        sw2 = jax.random.normal(ks[8], (HIDDEN, D_MODEL), dtype=jnp.float32) * s
        sb2 = jax.random.normal(ks[9], (D_MODEL,), dtype=jnp.float32) * s
        return {'x': x, 'gate_w': gate_w, 'w1': w1, 'b1': b1, 'w2': w2, 'b2': b2, 'sw1': sw1, 'sb1': sb1, 'sw2': sw2, 'sb2': sb2}
    _L0_ffn_in = _L0_ffn_setup()
    _L0_c = _w((lambda *s: np.random.randn(*s).astype(np.float32) * 0.05)(8, 128))
    _L0_wmod = _w((lambda *s: np.random.randn(*s).astype(np.float32) * 0.05)(128, 6 * 128) * 128 ** (-0.5))
    _d = {'L0_attn_x': _L0_attn_in['x'], 'L0_attn_Wq': _L0_attn_in['Wq'], 'L0_attn_Wk': _L0_attn_in['Wk'], 'L0_attn_Wv': _L0_attn_in['Wv'], 'L0_attn_Wo': _L0_attn_in['Wo'], 'L0_attn_rel_emb': _L0_attn_in['rel_emb'], 'L0_ffn_gate_w': _L0_ffn_in['gate_w'], 'L0_ffn_w1': _L0_ffn_in['w1'], 'L0_ffn_b1': _L0_ffn_in['b1'], 'L0_ffn_w2': _L0_ffn_in['w2'], 'L0_ffn_b2': _L0_ffn_in['b2'], 'L0_ffn_sw1': _L0_ffn_in['sw1'], 'L0_ffn_sb1': _L0_ffn_in['sb1'], 'L0_ffn_sw2': _L0_ffn_in['sw2'], 'L0_ffn_sb2': _L0_ffn_in['sb2'], 'L0_c': _L0_c, 'L0_wmod': _L0_wmod}
    _x0 = _d['L0_attn_x']
    _d['L0_attn_x'] = jax.random.normal(jax.random.fold_in(jax.random.key(seed), 1), (8, 512, 128), dtype=_x0.dtype)
    del _x0
    return _d

def reference(L0_attn_x, L0_attn_Wq, L0_attn_Wk, L0_attn_Wv, L0_attn_Wo, L0_attn_rel_emb, L0_ffn_gate_w, L0_ffn_w1, L0_ffn_b1, L0_ffn_w2, L0_ffn_b2, L0_ffn_sw1, L0_ffn_sb1, L0_ffn_sw2, L0_ffn_sb2, L0_c, L0_wmod):

    def _L0_attn_ref(x, Wq, Wk, Wv, Wo, rel_emb):
        import math
        import jax, jax.numpy as jnp
        import numpy as np
        N_HEADS = 16
        D_KV = 64
        NUM_BUCKETS = 32
        MAX_DISTANCE = 128

        def _relative_position_bucket(relative_position, num_buckets=NUM_BUCKETS, max_distance=MAX_DISTANCE):
            num_buckets //= 2
            n = -relative_position
            ret = (n < 0).astype(jnp.int32) * num_buckets
            n = jnp.abs(n)
            max_exact = num_buckets // 2
            is_small = n < max_exact
            val_if_large = max_exact + (jnp.log(jnp.maximum(n, 1).astype(jnp.float32) / max_exact) / math.log(max_distance / max_exact) * (num_buckets - max_exact)).astype(jnp.int32)
            val_if_large = jnp.minimum(val_if_large, num_buckets - 1)
            return ret + jnp.where(is_small, n, val_if_large)
        B, S, D = x.shape
        H, Dk = (N_HEADS, D_KV)

        def shape(t):
            return t.reshape(B, S, H, Dk).transpose(0, 2, 1, 3)
        q = shape(x @ Wq)
        k = shape(x @ Wk)
        v = shape(x @ Wv)
        scores = jnp.einsum('bhqd,bhkd->bhqk', q, k)
        ctx_pos = jnp.arange(S)[:, None]
        mem_pos = jnp.arange(S)[None, :]
        rp_bucket = _relative_position_bucket(mem_pos - ctx_pos)
        position_bias = rel_emb[rp_bucket].transpose(2, 0, 1)[None]
        weights = jax.nn.softmax(scores + position_bias, axis=-1)
        context = jnp.einsum('bhqk,bhkd->bhqd', weights, v)
        context = context.transpose(0, 2, 1, 3).reshape(B, S, H * Dk)
        return context @ Wo

    def _L0_ffn_ref(x, gate_w, w1, b1, w2, b2, sw1, sb1, sw2, sb2):
        import jax, jax.numpy as jnp
        import numpy as np
        D_MODEL = 128
        HIDDEN = 512
        N_ROUTING = 2
        B, S, D = x.shape
        xf = x.reshape(-1, D)
        gate_scores = xf @ gate_w.T
        gate_probs = jax.nn.softmax(gate_scores, axis=-1)
        top1 = jnp.argmax(gate_probs, axis=-1)
        one_hot = jax.nn.one_hot(top1, N_ROUTING, dtype=xf.dtype)
        masked = xf[None, :, :] * one_hot.T[:, :, None]
        h = jax.nn.relu(jnp.einsum('end,edh->enh', masked, w1) + b1[:, None, :])
        expert_out = jnp.einsum('enh,ehd->end', h, w2) + b2[:, None, :]
        routing_output = expert_out.sum(axis=0)
        shared = jax.nn.relu(xf @ sw1 + sb1) @ sw2 + sb2
        return (routing_output + shared).reshape(B, S, D)
    x = L0_attn_x
    mod = (_silu(L0_c) @ L0_wmod).reshape(L0_c.shape[0], 6, 1, -1)
    sa, ca, ga, sb, cb, gb = (mod[:, 0], mod[:, 1], mod[:, 2], mod[:, 3], mod[:, 4], mod[:, 5])
    ga = (2 * (ga >= 0) - 1) * jnp.maximum(jnp.abs(ga), 0.25)
    gb = (2 * (gb >= 0) - 1) * jnp.maximum(jnp.abs(gb), 0.25)
    h = _layernorm(x, axis=-1) * (1 + ca) + sa
    x = x + ga * _L0_attn_ref(h, L0_attn_Wq, L0_attn_Wk, L0_attn_Wv, L0_attn_Wo, L0_attn_rel_emb)
    h = _layernorm(x, axis=-1) * (1 + cb) + sb
    x = x + gb * _L0_ffn_ref(h, L0_ffn_gate_w, L0_ffn_w1, L0_ffn_b1, L0_ffn_w2, L0_ffn_b2, L0_ffn_sw1, L0_ffn_sb1, L0_ffn_sw2, L0_ffn_sb2)
    return x

_drawn_inputs = setup_inputs


def setup_inputs(seed=0):
    import zlib

    import numpy as np

    out = dict(_drawn_inputs(seed))
    spreads = {}
    factors = {'L0_attn_Wq': 8.0,
     'L0_attn_Wk': 8.0,
     'L0_attn_Wv': 8.0,
     'L0_attn_Wo': 8.0,
     'L0_attn_rel_emb': 8.0,
     'L0_ffn_gate_w': 4.448,
     'L0_ffn_w1': 3.794,
     'L0_ffn_b1': 22.677,
     'L0_ffn_w2': 3.107,
     'L0_ffn_b2': 7.428,
     'L0_ffn_sw1': 3.837,
     'L0_ffn_sb1': 29.946,
     'L0_ffn_sw2': 3.105,
     'L0_ffn_sb2': 24.48}
    for name, (base, spread) in spreads.items():
        noise = np.random.default_rng([zlib.crc32(name.encode()), seed]).standard_normal(out[name].shape)
        drawn = base * np.exp(spread * noise) if base else spread * noise
        out[name] = jnp.asarray(drawn.astype(out[name].dtype))
    for name, factor in factors.items():
        out[name] = (out[name] * factor).astype(out[name].dtype)
    return out
```

```python
from contextlib import ExitStack

import numpy as np

import concourse.bass as bass
from concourse import mybir

F32 = mybir.dt.float32
F16 = mybir.dt.float16
BF16 = mybir.dt.bfloat16
ALU = mybir.AluOpType
ACT = mybir.ActivationFunctionType
AXX = mybir.AxisListType.X

P = 128
B, S, D = 8, 512, 128
H, DK = 16, 64
TPB = S // P
TILES = B * TPB
PAIRS = H // 2
ITERS = B * PAIRS
RING = 3
UNROLL = 6
LOOPS = (ITERS - 4) // UNROLL
HID, EXPERTS = 512, 3
HC = HID // P
CHUNKS = EXPERTS * HC
EPS = 1e-5
BUCKETS, EXACT = 32, 8
FAR = 91
BAND = 2 * FAR + P - 2
OFFS = 2 * (FAR + P - 2) + 1
M_ROW = DK
M_SCALE = 32.0
FAR_ROW = M_ROW + 1

WQ, WK, WV, WO = 0, 1024, 2048, 3072
W1 = 4096
W2 = W1 + EXPERTS * HID
WCOLS = W2 + EXPERTS * HC * D

POOL_LO = (3,)
DVE_LO = (0, 1, 2)


def band_of(kt):
    first = P * kt - FAR + 1
    q0, q1 = max(0, first), min(S, first + BAND)
    return q0, q1, q0 - first


def bucket_of(n):
    a = abs(n)
    b = a if a < EXACT else EXACT + sum(a * a >= 64 * 2 ** j for j in range(1, EXACT))
    return b + (BUCKETS // 2 if n < 0 else 0)


def shape_constants():
    onehot = np.zeros((BUCKETS, OFFS), np.float32)
    for m in range(OFFS):
        onehot[bucket_of(m - OFFS // 2), m] = 1
    select = np.zeros((BUCKETS, P), np.float32)
    rowmask = np.zeros((P, 3 + TPB), np.float32)
    indicator = np.zeros((P, S), np.float16)
    rowmask[M_ROW, 2] = M_SCALE
    rowmask[M_ROW, 3:] = 1
    q = np.arange(S)
    for j in range(TPB):
        for side in range(2):
            for part in range(2):
                r = FAR_ROW + 4 * j + 2 * side + part
                select[bucket_of(-FAR if side == 0 else FAR), r] = 1
                rowmask[r, part] = 1
                rowmask[r, 3 + j] = 1
                indicator[r] = (q <= P * j - FAR) if side == 0 else (q >= P * j + P - 1 + FAR)
    return {"ident": np.eye(P, dtype=np.float32), "onehot": onehot, "select": select,
            "rowmask": rowmask, "indicator": indicator}


def adaln_program(nc, ins, consts, out):
    x_d = ins["L0_attn_x"].rearrange("b s d -> (b s) d").rearrange("(t p) d -> p t d", p=P)
    out_d = out.rearrange("b s d -> (b s) d").rearrange("(t p) d -> p t d", p=P)
    bias_scratch = nc.dram_tensor("bias_scratch", (P, H, OFFS), F32, kind="Internal").ap()

    ctx = ExitStack()
    with ctx:
        ctx.enter_context(nc.allow_non_contiguous_dma(reason="small transposed vectors"))

        def sb(name, shape, dt=F32):
            return ctx.enter_context(nc.sbuf_tensor(name, shape, dt))

        def sem(name):
            return ctx.enter_context(nc.semaphore(name))

        bank = [ctx.enter_context(nc.psum_tensor(f"bank{i}", [P, 512], F32)) for i in range(8)]

        x = sb("x", [P, TILES * D])
        hT_hi = sb("hT_hi", [P, B * S], F16)
        hT_lo = sb("hT_lo", [P, B * S], F16)
        w_raw = sb("w_raw", [P, WCOLS])
        w_hi = sb("w_hi", [P, WCOLS], F16)
        w_lo = sb("w_lo", [P, WCOLS], F16)
        attn_T = w_raw[:, 0:B * S]
        k_lo = sb("k_lo", [P, H * S], F16)
        exp_bias = sb("exp_bias", [P, H * BAND])
        pair_hi = sb("pair_hi", [P, 2 * S], F16)
        pair_lo = sb("pair_lo", [P, 2 * S], F16)
        q_hilo = sb("q_hilo", [P, RING * 2 * S], F16)
        q_ext = sb("q_ext", [P, RING * 2 * S], F16)
        k_hihi = sb("k_hihi", [P, RING * 2 * S], F16)
        VP = DK + 2
        v_hi = sb("v_hi", [P, RING * 2 * TPB * VP], F16)
        v_lo = sb("v_lo", [P, RING * 2 * TPB * DK], F16)
        probs = sb("probs", [P, 2 * TPB * S])
        probs_lo = sb("probs_lo", [P, 2 * TPB * S], F16)
        row_max = sb("row_max", [P, 2 * TPB])
        max_row = sb("max_row", [TPB, 2 * P], F16)
        recip = sb("recip", [P, TPB])
        ctx_n = sb("ctx_n", [P, TPB * P])
        ctxT = sb("ctxT", [P, S])
        ctxT_lo = sb("ctxT_lo", [P, S], F16)
        attn_part = sb("attn_part", [P, S])
        ident = sb("ident_sb", [P, P])
        onehot = sb("onehot_sb", [BUCKETS, OFFS])
        select = sb("select_sb", [BUCKETS, P])
        rowmask = sb("rowmask_sb", [P, 3 + TPB])
        rel = sb("rel", [BUCKETS, H])
        rel_all = sb("rel_all", [P, BUCKETS * H])
        relT = sb("relT", [H, BUCKETS])
        rel_top = sb("rel_top", [P, H])
        relT_ntop = sb("relT_ntop", [H, 1])
        eb_row = sb("eb_row", [H, OFFS])
        far = sb("far", [P, 3 * H])
        far_hi = sb("far_hi", [P, H], F16)
        far_tile = sb("far_tile", [P, H * TPB])
        cT = sb("cT", [P, 3 * B])
        wmod = sb("wmod", [P, 6 * D])
        mod = sb("mod", [P, 6 * B])
        gates = sb("gates", [P, 2 * 4 * B])
        b1T = sb("b1T", [P, CHUNKS])
        b2T = sb("b2T", [P, EXPERTS + 2])
        b2g = sb("b2g", [P, B])
        gateT = sb("gateT", [P, 2])
        ones = sb("ones", [P, P])
        gate_hi = sb("gate_hi", [P, 2 * P], F16)
        gate_lo = sb("gate_lo", [P, 2 * P], F16)
        stats = sb("stats", [P, TILES * 6])
        mean_var = sb("mean_var", [P, TILES * 2])
        var_eps = sb("var_eps", [P, TILES])
        minus_half = sb("minus_half", [P, TILES])
        rstd = sb("rstd", [P, TILES])
        xn = probs[:, 0:2 * S]
        h32 = probs[:, 2 * S:4 * S]
        hid = probs[:, 4 * S:8 * S]
        hid_lo = probs_lo[:, 0:4 * S]
        xm = probs_lo[:, 4 * S:8 * S]
        moe_T = ctx_n
        x_out = q_hilo[:, :].bitcast(F32)

        def mod_col(i, b):
            return mod[:, bass.ds(i * B + b, 1)]

        (consts_in, x_in, small_in, attn_w_in, ffn_w_in, wmod_in, bias_out, bias_in, far_in, spread_a, spread_b,
         stored) = map(sem, ("consts_in", "x_in", "small_in", "attn_w_in", "ffn_w_in", "wmod_in", "bias_out",
                             "bias_in", "far_in", "spread_a", "spread_b", "stored"))
        mrow_in = [sem("mrow_in0"), sem("mrow_in1")]
        setup_dve = sem("setup_dve")
        setup_act = sem("setup_act")
        setup_pe = sem("setup_pe")
        w_hi_done, w_lo_done = sem("w_hi_done"), sem("w_lo_done")
        fills = sem("fills")
        far_rows = sem("far_rows")
        ln = [{k: sem(f"ln{ph}_{k}") for k in ("stats", "aggr", "eps", "rstd", "xn", "xT", "h32", "hi", "lo")}
              for ph in range(2)]
        (proj_done, scores_done, tops_done, top_done, topT_done, mrow_done, qkv_hi, qkv_lo, exp_done, band_done,
         lo_dve, lo_pool, pv_done, recip_done, norm_done, ctxT_done, ctx_out, ctx_lo, wo_done, wout_read,
         summed) = map(sem, ("proj_done", "scores_done", "tops_done", "top_done", "topT_done", "mrow_done", "qkv_hi",
                             "qkv_lo", "exp_done", "band_done", "lo_dve", "lo_pool", "pv_done", "recip_done",
                             "norm_done", "ctxT_done", "ctx_out", "ctx_lo", "wo_done", "wout_read", "summed"))
        attn_back, resid = sem("attn_back"), sem("resid")
        (gate_done, masked, up_done, hid_done, hid_lo_done, down_done, moe_done, moe_back, y_done) = map(
            sem, ("gate_done", "masked", "up_done", "hid_done", "hid_lo_done", "down_done", "moe_done", "moe_back",
                  "y_done"))

        block = ctx.enter_context(nc.Block())

        def st_bank(kt):
            return bank[kt % 2]
        def s_bank(t):
            return bank[2 + t % 2]
        PV, PROJ, TURN, WOUT = bank[4], bank[5], bank[6], bank[7]

        def slot(ring, hh):
            return (2 * ring + hh) * S

        def attention(eng, iteration):
            iteration(0, 0)
            iteration(1, 1)
            with eng.Fori(0, LOOPS) as j:
                for u in range(UNROLL):
                    iteration(UNROLL * j + 2 + u, 2 + u)
            iteration(ITERS - 2, ITERS - 2)
            iteration(ITERS - 1, ITERS - 1)

        def is_at(it, n):
            return isinstance(it, int) and it == n

        w_pieces = [
            (WQ, 1024, ins["L0_attn_Wq"]), (WK, 1024, ins["L0_attn_Wk"]), (WV, 1024, ins["L0_attn_Wv"]),
            (WO, 1024, ins["L0_attn_Wo"].rearrange("(g p) n -> p g n", p=P)),
            (W1, 1024, ins["L0_ffn_w1"].rearrange("e d h -> d e h")),
            (W1 + 1024, 512, ins["L0_ffn_sw1"]),
            (W2, 1024, ins["L0_ffn_w2"].rearrange("e (c p) d -> p (e c) d", p=P)),
            (W2 + 1024, 512, ins["L0_ffn_sw2"].rearrange("(c p) d -> p c d", p=P)),
        ]
        ATTN_PIECES = 4

        def w_part(t, o, n):
            if o in (WQ, WK):
                return t[:, o:o + n].rearrange("p (g d h) -> p g h d", h=2, d=DK)
            return t[:, o:o + n]

        def w_source(o, n):
            if o in (WQ, WK):
                return w_raw[:, o:o + n].rearrange("p (g h d) -> p g h d", h=2, d=DK)
            return w_raw[:, o:o + n]

        def w_view(o, n, src):
            t = w_raw[:, o:o + n]
            return t if len(src.shape) == 2 else t.rearrange("p (g n) -> p g n", n=src.shape[-1])

        @block.sync
        def _(sp):
            sp.dma_start(x[:, :].rearrange("p (t d) -> p t d", d=D), x_d).then_inc(x_in, 16)
            for o, n, src in w_pieces[:ATTN_PIECES]:
                sp.dma_start(w_view(o, n, src), src).then_inc(attn_w_in, 16)
            for o, n, src in w_pieces[ATTN_PIECES:]:
                sp.dma_start(w_view(o, n, src), src).then_inc(ffn_w_in, 16)
            sp.wait_ge(setup_act, 3)
            sp.dma_start(bias_scratch.rearrange("p h m -> h p m"),
                         eb_row[:, :].unsqueeze(1).to_broadcast([H, P, OFFS])).then_inc(bias_out, 16)
            sp.wait_ge(bias_out, 16)
            toeplitz = bass.AP(tensor=bias_scratch.tensor, offset=bias_scratch.offset + P - 1,
                               ap=[[H * OFFS - 1, P], [OFFS, H], [1, BAND]])
            sp.dma_start(exp_bias[:, :].rearrange("p (h c) -> p h c", h=H), toeplitz).then_inc(bias_in, 16)

            def max_row_in(n, ring, hh):
                sp.wait_ge(mrow_done, 2 * n + hh + 1)
                o = slot(ring, hh)
                sp.dma_start(q_ext[M_ROW:M_ROW + 1, o:o + S].rearrange("o (t c) -> o t c", c=P),
                             max_row[:, hh * P:hh * P + P]).then_inc(mrow_in[hh], 16)

            def spread(dst, src, done):
                sp.dma_start(dst.rearrange("p (h c) -> p h c", h=2), src).then_inc(done, 16)

            def spread_q(n, ring):
                o = slot(ring, 0)
                sp.wait_ge(qkv_hi, 3 * n + 1)
                spread(q_hilo[0:DK, o:o + 2 * S], pair_hi[:, 0:S], spread_a)
                spread(q_ext[0:DK, o:o + 2 * S], pair_hi[:, 0:S], spread_b)
                sp.wait_ge(qkv_lo, 3 * n + 1)
                spread(q_hilo[DK:P, o:o + 2 * S], pair_lo[:, 0:S], spread_a)

            def spread_k(n, ring):
                o = slot(ring, 0)
                sp.wait_ge(qkv_hi, 3 * n + 2)
                spread(k_hihi[0:DK, o:o + 2 * S], pair_hi[:, S:2 * S], spread_a)
                spread(k_hihi[DK:P, o:o + 2 * S], pair_hi[:, S:2 * S], spread_a)
                sp.wait_ge(qkv_lo, 3 * n + 2)
                at = (((n + PAIRS) << 1) & (2 * PAIRS - 2)) << 9
                spread(k_lo[0:DK, bass.ds(at, 2 * S)], pair_lo[:, S:2 * S], spread_b)

            def iteration(it, i):
                max_row_in(it, i % RING, 1)
                if not is_at(it, ITERS - 2) and not is_at(it, ITERS - 1):
                    spread_q(it + 2, (i + 2) % RING)
                    spread_k(it + 2, (i + 2) % RING)
                if not is_at(it, ITERS - 1):
                    max_row_in(it + 1, (i + 1) % RING, 0)

            sp.wait_ge(far_in, 16 * 2 * RING)
            spread_q(0, 0)
            spread_k(0, 0)
            max_row_in(0, 0, 0)
            spread_q(1, 1)
            spread_k(1, 1)
            attention(sp, iteration)

            with sp.Fori(0, B // 2) as j:
                for par in range(2):
                    b = 2 * j + par
                    sp.wait_ge(y_done, b + 1)
                    sp.dma_start(out_d[:, bass.ds(b * TPB, TPB), :],
                                 x_out[:, par * S:par * S + S].rearrange("p (t d) -> p t d", d=D)
                                 ).then_inc(stored, 16)
            sp.wait_ge(stored, 16 * B)

        @block.gpsimd
        def _(pool):
            pool.dma_start(cT[:, 0:B], ins["L0_c"].rearrange("b d -> d b")).then_inc(small_in, 16)
            pool.dma_start(rel[:, :], ins["L0_attn_rel_emb"]).then_inc(small_in, 16)
            pool.dma_start(relT[:, :], ins["L0_attn_rel_emb"].rearrange("n h -> h n")).then_inc(small_in, 16)
            pool.dma_start(rel_all[:, :].rearrange("p (n h) -> p n h", h=H),
                           bass.AP(tensor=ins["L0_attn_rel_emb"].tensor, offset=ins["L0_attn_rel_emb"].offset,
                                   ap=[[0, P], [H, BUCKETS], [1, H]])).then_inc(small_in, 16)
            pool.dma_start(wmod[:, :], ins["L0_wmod"]).then_inc(wmod_in, 16)
            pool.dma_start(b1T[:, 0:2 * HC].rearrange("p (e c) -> p e c", e=2),
                           ins["L0_ffn_b1"].rearrange("e (c p) -> p e c", p=P)).then_inc(small_in, 16)
            pool.dma_start(b1T[:, 2 * HC:3 * HC],
                           ins["L0_ffn_sb1"].rearrange("(c p) -> p c", p=P)).then_inc(small_in, 16)
            pool.dma_start(b2T[:, 0:2], ins["L0_ffn_b2"].rearrange("e p -> p e")).then_inc(small_in, 16)
            pool.dma_start(b2T[:, 2:3], ins["L0_ffn_sb2"].rearrange("(p o) -> p o", o=1)).then_inc(small_in, 16)
            pool.dma_start(gateT[:, :], ins["L0_ffn_gate_w"].rearrange("e p -> p e")).then_inc(small_in, 16)
            pool.memset(minus_half[:, :], -0.5).then_inc(fills, 1)
            pool.memset(v_hi[:, :], 1.0).then_inc(fills, 1)
            pool.memset(ones[:, :], 1.0).then_inc(fills, 1)

            def layernorm(ph):
                s = ln[ph]
                pool.wait_ge(s["eps"], 1)
                pool.tensor_tensor(rstd[:, :], var_eps[:, :], minus_half[:, :], ALU.pow).then_inc(s["rstd"], 1)
                with pool.Fori(0, B // 2) as j:
                    for par in range(2):
                        b = 2 * j + par
                        pool.wait_ge(s["hi"], b + 1)
                        pool.tensor_tensor(hT_lo[:, bass.ds(b * S, S)], h32[:, par * S:par * S + S],
                                           hT_hi[:, bass.ds(b * S, S)], ALU.subtract).then_inc(s["lo"], 1)

            pool.wait_ge(fills, 1)
            layernorm(0)
            pool.wait_ge(w_lo_done, len(w_pieces))
            pool.memset(attn_T, 0.0).then_inc(summed, 1)
            pool.wait_ge(bias_in, 16)

            def numerators(n, hh):
                g2 = ((n & (PAIRS - 1)) * 2 + hh) * BAND
                for kt in range(TPB):
                    q0, q1, c0 = band_of(kt)
                    o = (hh * TPB + kt) * S
                    pool.wait_ge(exp_done, 8 * n + 4 * hh + kt + 1)
                    at = ((g2 << kt) >> kt) + c0
                    pool.tensor_tensor(probs[:, o + q0:o + q1], probs[:, o + q0:o + q1],
                                       exp_bias[:, bass.ds(at, q1 - q0)], ALU.mult).then_inc(band_done, 1)
                    if kt in POOL_LO:
                        pool.wait_ge(band_done, 8 * n + 4 * hh + kt + 1)
                        pool.tensor_tensor(probs_lo[:, o:o + S], probs[:, o:o + S],
                                           probs[:, o:o + S].bitcast(BF16)[:, 1:2 * S:2],
                                           ALU.subtract).then_inc(lo_pool, 1)

            def context_lo(n):
                pool.wait_ge(ctx_out, n + 1)
                pool.tensor_tensor(ctxT_lo[:, :], ctxT[:, :], ctxT[:, :].bitcast(BF16)[:, 1:2 * S:2],
                                   ALU.subtract).then_inc(ctx_lo, 1)

            def add_pairs(m):
                y = attn_T[:, bass.ds(((m >> 2) & (B - 1)) * S, S)]
                pool.wait_ge(wout_read, m + 2)
                pool.wait_ge(summed, m + 1)
                pool.tensor_tensor(y, y, attn_part[:, :], ALU.add).then_inc(summed, 1)

            def iteration(it, i):
                if not is_at(it, 0) and not is_at(it, 1):
                    context_lo(it - 2)
                numerators(it, 0)
                numerators(it, 1)
                if i % 2 == 1 and not is_at(it, 1):
                    add_pairs(it // 2 - 1 if isinstance(it, int) else (it >> 1) - 1)

            attention(pool, iteration)
            context_lo(ITERS - 2)
            context_lo(ITERS - 1)
            add_pairs(ITERS // 2 - 1)
            layernorm(1)

        @block.scalar
        def _(act):
            act.dma_start(ident[:, :], consts["ident"]).then_inc(consts_in, 16)
            act.dma_start(onehot[:, :], consts["onehot"]).then_inc(consts_in, 16)
            act.dma_start(select[:, :], consts["select"]).then_inc(consts_in, 16)
            act.dma_start(rowmask[:, :], consts["rowmask"]).then_inc(consts_in, 16)
            for s in range(2 * RING):
                act.dma_start(q_ext[DK:P, s * S:s * S + S], consts["indicator"][DK:P, :]).then_inc(far_in, 16)

            act.wait_ge(small_in, 16 * 9)
            act.activation(cT[:, B:2 * B], cT[:, 0:B], ACT.Exp, scale=-1.0).then_inc(setup_act, 1)
            act.wait_ge(setup_pe, 1)
            act.activation(mod[:, :], PROJ[:, 0:6 * B], ACT.Copy).then_inc(setup_act, 1)
            act.wait_ge(setup_pe, 2)
            act.wait_ge(setup_dve, 4)
            act.activation(eb_row[:, :], TURN[0:H, 0:OFFS], ACT.Exp, bias=relT_ntop[:, 0:1]).then_inc(setup_act, 1)

            def layernorm(ph):
                s = ln[ph]
                shift, scale = (0, 1) if ph == 0 else (3, 4)
                with act.Fori(0, B // 2) as j:
                    for par in range(2):
                        b = 2 * j + par
                        act.wait_ge(s["xT"], b + 1)
                        act.wait_ge(s["lo"], 2 * j)
                        act.activation(h32[:, par * S:par * S + S], bank[par][:, :], ACT.Identity,
                                       bias=mod_col(shift, b), scale=mod_col(scale, b)).then_inc(s["h32"], 1)
                        act.wait_ge(s["h32"], b + 1)
                        act.activation(hT_hi[:, bass.ds(b * S, S)], h32[:, par * S:par * S + S],
                                       ACT.Copy).then_inc(s["hi"], 1)

            act.wait_ge(attn_w_in, 16 * ATTN_PIECES)
            for o, n, _ in w_pieces[:ATTN_PIECES]:
                act.activation(w_part(w_hi, o, n), w_source(o, n), ACT.Copy).then_inc(w_hi_done, 1)
            act.wait_ge(setup_dve, 7)
            layernorm(0)
            act.wait_ge(ffn_w_in, 16 * (len(w_pieces) - ATTN_PIECES))
            for o, n, _ in w_pieces[ATTN_PIECES:]:
                act.activation(w_part(w_hi, o, n), w_source(o, n), ACT.Copy).then_inc(w_hi_done, 1)
            act.wait_ge(setup_dve, 12)
            act.activation(k_lo[DK:P, :].rearrange("p (a c) -> p a c", c=P),
                           far_tile[DK:P, :].unsqueeze(2).to_broadcast([DK, H * TPB, P]),
                           ACT.Copy).then_inc(far_rows, 1)

            def exponentials(n, hh, kts):
                for kt in kts:
                    if kt == 0 and not (isinstance(n, int) and n == 0):
                        act.wait_ge(pv_done, 2 * n - 1 + hh)
                    o = (hh * TPB + kt) * S
                    act.wait_ge(scores_done, 8 * n + 4 * hh + kt + 1)
                    act.activation(probs[:, o:o + S], st_bank(kt)[:, :], ACT.Exp).then_inc(exp_done, 1)

            def pair_hi_part(n, k):
                act.wait_ge(proj_done, 3 * n + k + 1)
                if not (isinstance(n, int) and n == 0):
                    act.wait_ge(spread_a, 64 * n)
                    act.wait_ge(spread_b, 32 * n)
                act.activation(pair_hi[:, k * S:k * S + S], PROJ[:, :], ACT.Copy).then_inc(qkv_hi, 1)

            def v_hi_part(n, ring):
                act.wait_ge(proj_done, 3 * n + 3)
                o = ring * 2 * TPB * VP
                act.activation(v_hi[:, o:o + 2 * TPB * VP].rearrange("p (a c) -> p a c", c=VP)[:, :, 0:DK],
                               PROJ[:, :].rearrange("p (a c) -> p a c", c=DK), ACT.Copy).then_inc(qkv_hi, 1)

            def max_row_out(n, hh):
                act.wait_ge(topT_done, 2 * n + hh + 1)
                if not (isinstance(n, int) and n == 0):
                    act.wait_ge(mrow_in[hh], 16 * n)
                act.activation(max_row[:, hh * P:hh * P + P], TURN[0:TPB, 0:P], ACT.Copy,
                               scale=-1.0 / M_SCALE).then_inc(mrow_done, 1)

            def context_out(n):
                act.wait_ge(ctxT_done, n + 1)
                act.activation(ctxT[:, :], TURN[:, :], ACT.Copy).then_inc(ctx_out, 1)

            def attn_part_out(m):
                act.wait_ge(wo_done, 2 * m + 2)
                act.wait_ge(summed, m + 1)
                act.activation(attn_part[:, :], WOUT[:, :], ACT.Copy,
                               scale=gates[:, bass.ds((m >> 2) & (B - 1), 1)]).then_inc(wout_read, 1)

            def iteration(it, i):
                project, rate = not is_at(it, ITERS - 2) and not is_at(it, ITERS - 1), not is_at(it, ITERS - 1)
                exponentials(it, 0, (0, 1))
                if project:
                    pair_hi_part(it + 2, 0)
                exponentials(it, 0, (2, 3))
                max_row_out(it, 1)
                if project:
                    pair_hi_part(it + 2, 1)
                exponentials(it, 1, (0, 1))
                exponentials(it, 1, (2, 3))
                if i % 2 == 1 and not is_at(it, 1):
                    attn_part_out(it // 2 - 1 if isinstance(it, int) else (it >> 1) - 1)
                if rate:
                    max_row_out(it + 1, 0)
                if project:
                    v_hi_part(it + 2, (i + 2) % RING)
                if not is_at(it, 0):
                    context_out(it - 1)

            pair_hi_part(0, 0)
            pair_hi_part(0, 1)
            v_hi_part(0, 0)
            max_row_out(0, 0)
            pair_hi_part(1, 0)
            pair_hi_part(1, 1)
            v_hi_part(1, 1)
            attention(act, iteration)
            context_out(ITERS - 1)
            attn_part_out(ITERS // 2 - 1)

            layernorm(1)

            with act.Fori(0, B // 2) as j:
                for par in range(2):
                    b = 2 * j + par
                    for c in range(CHUNKS):
                        e = (2, 0, 1)[c // HC]
                        act.wait_ge(up_done, CHUNKS * b + c + 1)
                        if c >= 4:
                            act.wait_ge(down_done, CHUNKS * b + c - 3)
                        else:
                            act.wait_ge(down_done, CHUNKS * b)
                        act.activation(hid[:, (c % 4) * S:(c % 4) * S + S], bank[c % 2][:, :], ACT.Relu,
                                       bias=b1T[:, e * HC + c % HC:e * HC + c % HC + 1]).then_inc(hid_done, 1)
                    act.wait_ge(down_done, CHUNKS * b + CHUNKS)
                    act.wait_ge(moe_back, b)
                    act.activation(moe_T[:, :], bank[2][:, :], ACT.Identity, bias=b2g[:, bass.ds(b, 1)],
                                   scale=gates[:, bass.ds(4 * B + b, 1)]).then_inc(moe_done, 1)

        @block.vector
        def _(dve):
            dve.wait_ge(small_in, 16 * 9)
            dve.reduce_max(rel_top[:, :], rel_all[:, :].rearrange("p (n h) -> p h n", h=H), AXX).then_inc(setup_dve, 1)
            dve.reduce_max(relT_ntop[:, :], relT[:, :], AXX).then_inc(setup_dve, 1)
            dve.wait_ge(setup_dve, 2)
            dve.tensor_scalar(relT_ntop[:, :], relT_ntop[:, :], -1.0, None, ALU.mult).then_inc(setup_dve, 1)
            dve.wait_ge(setup_act, 1)
            dve.tensor_scalar(cT[:, B:2 * B], cT[:, B:2 * B], 1.0, None, ALU.add).then_inc(setup_dve, 1)
            dve.wait_ge(setup_dve, 4)
            dve.reciprocal(cT[:, 2 * B:3 * B], cT[:, B:2 * B]).then_inc(setup_dve, 1)
            dve.wait_ge(setup_dve, 5)
            dve.tensor_tensor(cT[:, B:2 * B], cT[:, 0:B], cT[:, 2 * B:3 * B], ALU.mult).then_inc(setup_dve, 1)
            dve.wait_ge(setup_act, 2)
            dve.tensor_scalar(mod[:, B:2 * B], mod[:, B:2 * B], 1.0, None, ALU.add)
            dve.tensor_scalar(mod[:, 4 * B:5 * B], mod[:, 4 * B:5 * B], 1.0, None, ALU.add)
            for k, i in enumerate((2, 5)):
                raw = mod[:, i * B:i * B + B]
                o = k * 4 * B
                dve.tensor_scalar(gates[:, o + B:o + 2 * B], raw, -1.0, None, ALU.mult)
                dve.tensor_scalar(gates[:, o + 2 * B:o + 3 * B], raw, 0.0, 2.0, ALU.is_ge, ALU.mult)
                dve.drain()
                dve.tensor_tensor(gates[:, o + B:o + 2 * B], gates[:, o + B:o + 2 * B], raw, ALU.max)
                dve.tensor_scalar(gates[:, o + 2 * B:o + 3 * B], gates[:, o + 2 * B:o + 3 * B], -1.0, None, ALU.add)
                dve.drain()
                dve.tensor_scalar(gates[:, o + B:o + 2 * B], gates[:, o + B:o + 2 * B], 0.25, None, ALU.max)
                dve.drain()
                last = dve.tensor_tensor(gates[:, o:o + B], gates[:, o + B:o + 2 * B],
                                         gates[:, o + 2 * B:o + 3 * B], ALU.mult)
            last.then_inc(setup_dve, 1)

            def layernorm(ph):
                s = ln[ph]
                with dve.Fori(0, B // 2) as j:
                    for par in range(2):
                        b = 2 * j + par
                        xb = x[:, bass.ds(b * S, S)]
                        if ph == 1:
                            dve.wait_ge(attn_back, b + 1)
                            dve.tensor_tensor(xb, xb, bank[2 + par][:, :], ALU.add).then_inc(resid, 1)
                            dve.wait_ge(resid, b + 1)
                        for t in range(TPB):
                            dve.bn_stats(stats[:, bass.ds((b * TPB + t) * 6, 6)],
                                         x[:, bass.ds(b * S + t * P, P)]).then_inc(s["stats"], 1)
                dve.wait_ge(s["stats"], TILES)
                for n in range(TILES):
                    dve.bn_aggr(mean_var[:, 2 * n:2 * n + 2], stats[:, 6 * n:6 * n + 6]).then_inc(s["aggr"], 1)
                dve.wait_ge(s["aggr"], TILES)
                dve.tensor_scalar(var_eps[:, :], mean_var[:, 1:2 * TILES:2], EPS, None, ALU.add).then_inc(s["eps"], 1)
                dve.wait_ge(s["rstd"], 1)
                with dve.Fori(0, B // 2) as j:
                    for par in range(2):
                        b = 2 * j + par
                        dve.wait_ge(s["xT"], 2 * j)
                        for t in range(TPB):
                            n = b * TPB + t
                            dve.tensor_scalar(xn[:, par * S + t * P:par * S + t * P + P],
                                              x[:, bass.ds(b * S + t * P, P)], mean_var[:, bass.ds(2 * n, 1)],
                                              rstd[:, bass.ds(n, 1)], ALU.subtract, ALU.mult).then_inc(s["xn"], 1)

            dve.wait_ge(x_in, 16)
            layernorm(0)
            for k, (o, n, _) in enumerate(w_pieces[:ATTN_PIECES]):
                dve.wait_ge(w_hi_done, k + 1)
                dve.tensor_tensor(w_part(w_lo, o, n), w_source(o, n), w_part(w_hi, o, n),
                                  ALU.subtract).then_inc(w_lo_done, 1)
            dve.wait_ge(setup_pe, 3)
            dve.wait_ge(consts_in, 16 * 4)
            dve.tensor_tensor(far[:, 0:H], WOUT[:, 0:H], rel_top[:, :], ALU.subtract).then_inc(setup_dve, 1)
            dve.wait_ge(setup_dve, 8)
            dve.tensor_copy(far_hi[:, :], far[:, 0:H]).then_inc(setup_dve, 1)
            dve.wait_ge(setup_dve, 9)
            dve.tensor_tensor(far[:, H:2 * H], far[:, 0:H], far_hi[:, :], ALU.subtract).then_inc(wout_read, 1)
            dve.tensor_scalar(far[:, 2 * H:3 * H], far_hi[:, :], rowmask[:, 0:1], rowmask[:, 2:3],
                              ALU.mult, ALU.add).then_inc(setup_dve, 1)
            dve.wait_ge(setup_dve, 10)
            dve.scalar_tensor_tensor(far[:, 0:H], far[:, H:2 * H], rowmask[:, 1:2], far[:, 2 * H:3 * H],
                                     ALU.mult, ALU.add).then_inc(setup_dve, 1)
            dve.wait_ge(setup_dve, 11)
            dve.tensor_tensor(far_tile[:, :].rearrange("p (h j) -> p h j", j=TPB),
                              far[:, 0:H].unsqueeze(2).to_broadcast([P, H, TPB]),
                              rowmask[:, 3:3 + TPB].unsqueeze(1).to_broadcast([P, H, TPB]),
                              ALU.mult).then_inc(setup_dve, 1)
            dve.wait_ge(fills, 3)
            for e in range(2):
                sign = -1.0 if e == 0 else 1.0
                dve.tensor_scalar(ctx_n[:, e * P:e * P + P], ones[:, :], gateT[:, e:e + 1], sign, ALU.mult, ALU.mult)
            dve.drain()
            dve.tensor_copy(gate_hi[:, :], ctx_n[:, 0:2 * P])
            dve.drain()
            dve.tensor_tensor(gate_lo[:, :], ctx_n[:, 0:2 * P], gate_hi[:, :], ALU.subtract)
            dve.tensor_tensor(b2T[:, 3:4], b2T[:, 0:1], b2T[:, 1:2], ALU.add)
            dve.drain()
            dve.tensor_tensor(b2T[:, 4:5], b2T[:, 3:4], b2T[:, 2:3], ALU.add)
            dve.drain()
            dve.tensor_scalar(b2g[:, :], gates[:, 4 * B:5 * B], b2T[:, 4:5], None, ALU.mult).then_inc(setup_dve, 1)
            for k, (o, n, _) in enumerate(w_pieces[ATTN_PIECES:]):
                dve.wait_ge(w_hi_done, ATTN_PIECES + k + 1)
                dve.tensor_tensor(w_part(w_lo, o, n), w_source(o, n), w_part(w_hi, o, n),
                                  ALU.subtract).then_inc(w_lo_done, 1)

            def top(n, hh, t):
                if t == 0 and not (isinstance(n, int) and n == 0):
                    dve.wait_ge(topT_done, 2 * n - 1 + hh)
                dve.wait_ge(tops_done, 8 * n + 4 * hh + t + 1)
                dve.reduce_max(row_max[:, hh * TPB + t:hh * TPB + t + 1], s_bank(t)[:, :], AXX).then_inc(top_done, 1)

            def lo(n, hh, kt):
                if kt in POOL_LO:
                    return
                o = (hh * TPB + kt) * S
                dve.wait_ge(band_done, 8 * n + 4 * hh + kt + 1)
                dve.tensor_tensor(probs_lo[:, o:o + S], probs[:, o:o + S],
                                  probs[:, o:o + S].bitcast(BF16)[:, 1:2 * S:2], ALU.subtract).then_inc(lo_dve, 1)

            def pair_lo_part(n, k):
                dve.wait_ge(qkv_hi, 3 * n + k + 1)
                dve.tensor_tensor(pair_lo[:, k * S:k * S + S], PROJ[:, :], pair_hi[:, k * S:k * S + S],
                                  ALU.subtract).then_inc(qkv_lo, 1)

            def v_lo_part(n, ring):
                dve.wait_ge(qkv_hi, 3 * n + 3)
                o, ol = ring * 2 * TPB * VP, ring * 2 * TPB * DK
                dve.tensor_tensor(v_lo[:, ol:ol + 2 * TPB * DK].rearrange("p (a c) -> p a c", c=DK),
                                  PROJ[:, :].rearrange("p (a c) -> p a c", c=DK),
                                  v_hi[:, o:o + 2 * TPB * VP].rearrange("p (a c) -> p a c", c=VP)[:, :, 0:DK],
                                  ALU.subtract).then_inc(qkv_lo, 1)

            def normalise(n, hh):
                pvv = PV[:, 0:TPB * (DK + 1)].rearrange("p (t c) -> p t c", c=DK + 1)
                dve.wait_ge(pv_done, 2 * n + hh + 1)
                dve.reciprocal(recip[:, :].unsqueeze(2), pvv[:, :, DK:DK + 1]).then_inc(recip_done, 1)
                dve.wait_ge(recip_done, 2 * n + hh + 1)
                if hh == 0 and not is_at(n, 0):
                    dve.wait_ge(ctxT_done, n)
                dve.tensor_tensor(ctx_n[:, :].rearrange("p (t c) -> p t c", c=P)[:, :, hh * DK:hh * DK + DK],
                                  pvv[:, :, 0:DK], recip[:, :].unsqueeze(2).to_broadcast([P, TPB, DK]),
                                  ALU.mult).then_inc(norm_done, 1)

            def iteration(it, i):
                project, rate = not is_at(it, ITERS - 2) and not is_at(it, ITERS - 1), not is_at(it, ITERS - 1)
                top(it, 1, 0)
                top(it, 1, 1)
                if rate:
                    v_lo_part(it + 1, (i + 1) % RING)
                top(it, 1, 2)
                top(it, 1, 3)
                if not is_at(it, 0):
                    normalise(it - 1, 0)
                if project:
                    pair_lo_part(it + 2, 0)
                for kt in DVE_LO:
                    lo(it, 0, kt)
                if rate:
                    top(it + 1, 0, 0)
                    top(it + 1, 0, 1)
                if project:
                    pair_lo_part(it + 2, 1)
                if rate:
                    top(it + 1, 0, 2)
                    top(it + 1, 0, 3)
                if not is_at(it, 0):
                    normalise(it - 1, 1)
                for kt in DVE_LO:
                    lo(it, 1, kt)

            pair_lo_part(0, 0)
            pair_lo_part(0, 1)
            v_lo_part(0, 0)
            for t in range(TPB):
                top(0, 0, t)
            pair_lo_part(1, 0)
            pair_lo_part(1, 1)
            attention(dve, iteration)
            normalise(ITERS - 1, 0)
            normalise(ITERS - 1, 1)

            layernorm(1)

            with dve.Fori(0, B // 2) as j:
                for par in range(2):
                    b = 2 * j + par
                    dve.wait_ge(gate_done, b + 1)
                    for e in range(2):
                        for k, src in enumerate((hT_hi, hT_lo)):
                            o = (2 * e + k) * S
                            dve.scalar_tensor_tensor(xm[:, o:o + S], bank[3][:, :], 0.0,
                                                     src[:, bass.ds(b * S, S)],
                                                     ALU.is_gt if e == 1 else ALU.is_le,
                                                     ALU.mult).then_inc(masked, 1)
                    for c in range(CHUNKS):
                        o = (c % 4) * S
                        dve.wait_ge(hid_done, CHUNKS * b + c + 1)
                        dve.tensor_tensor(hid_lo[:, o:o + S], hid[:, o:o + S],
                                          hid[:, o:o + S].bitcast(BF16)[:, 1:2 * S:2],
                                          ALU.subtract).then_inc(hid_lo_done, 1)
                    dve.wait_ge(moe_back, b + 1)
                    dve.wait_ge(stored, 32 * j)
                    dve.tensor_tensor(x_out[:, par * S:par * S + S], x[:, bass.ds(b * S, S)], bank[4][:, :],
                                      ALU.add).then_inc(y_done, 1)

        @block.tensor
        def _(pe):
            pe.wait_ge(wmod_in, 16)
            pe.wait_ge(setup_dve, 6)
            for i in range(6):
                mm = pe.matmul(PROJ[:, i * B:i * B + B], wmod[:, i * D:i * D + D], cT[:, B:2 * B],
                               start=True, stop=True)
            mm.then_inc(setup_pe, 1)
            pe.wait_ge(consts_in, 16 * 4)
            pe.matmul(TURN[0:H, 0:OFFS], rel[:, :], onehot[:, :], start=True, stop=True).then_inc(setup_pe, 1)
            pe.matmul(WOUT[:, 0:H], select[:, :], rel[:, :], start=True, stop=True).then_inc(setup_pe, 1)

            def layernorm(ph):
                s = ln[ph]
                with pe.Fori(0, B // 2) as j:
                    for par in range(2):
                        b = 2 * j + par
                        pe.wait_ge(s["h32"], 2 * j)
                        pe.wait_ge(s["xn"], TPB * b + TPB)
                        for t in range(TPB):
                            o = par * S + t * P
                            mm = pe.transpose(bank[par][:, t * P:t * P + P], xn[:, o:o + P], ident[:, :])
                        mm.then_inc(s["xT"], 1)

            layernorm(0)

            def q_or_k(n, w, count):
                b, g = (n >> 3) & (B - 1), n & (PAIRS - 1)
                if not (isinstance(n, int) and n == 0 and count == 0):
                    pe.wait_ge(qkv_lo, 3 * n + count)
                h_hi, h_lo = hT_hi[:, bass.ds(b * S, S)], hT_lo[:, bass.ds(b * S, S)]
                pe.matmul(PROJ[:, :], w_hi[:, bass.ds(w + g * P, P)], h_hi, start=True, stop=False)
                pe.matmul(PROJ[:, :], w_lo[:, bass.ds(w + g * P, P)], h_hi, start=False, stop=False)
                pe.matmul(PROJ[:, :], w_hi[:, bass.ds(w + g * P, P)], h_lo, start=False,
                          stop=True).then_inc(proj_done, 1)

            def v_proj(n):
                b, g = (n >> 3) & (B - 1), n & (PAIRS - 1)
                pe.wait_ge(qkv_lo, 3 * n + 2)
                wv_hi, wv_lo = w_hi[:, bass.ds(WV + g * P, P)], w_lo[:, bass.ds(WV + g * P, P)]
                for t in range(TPB):
                    o = PROJ[:, t * P:t * P + P]
                    h_hi, h_lo = hT_hi[:, bass.ds(b * S + t * P, P)], hT_lo[:, bass.ds(b * S + t * P, P)]
                    pe.matmul(o, h_hi, wv_hi, start=True, stop=False)
                    pe.matmul(o, h_hi, wv_lo, start=False, stop=False)
                    mm = pe.matmul(o, h_lo, wv_hi, start=False, stop=True)
                mm.then_inc(proj_done, 1)

            def rough_scores(n, ring, hh, t):
                idx = 8 * n + 4 * hh + t
                o = slot(ring, hh)
                if not (isinstance(n, int) and n == 0) or hh or t >= 2:
                    pe.wait_ge(top_done, idx - 1)
                if hh == 0 and t == 0:
                    pe.wait_ge(spread_a, 64 * n + 64)
                pe.matmul(s_bank(t)[:, :], q_hilo[:, o + t * P:o + t * P + P], k_hihi[:, o:o + S],
                          start=True, stop=True).then_inc(tops_done, 1)

            def scores(n, ring, hh, kt):
                idx = 8 * n + 4 * hh + kt
                o = slot(ring, hh)
                if not (isinstance(n, int) and n == 0) or hh or kt >= 2:
                    pe.wait_ge(exp_done, idx - 1)
                pe.matmul(st_bank(kt)[:, :], k_hihi[:, o + kt * P:o + kt * P + P], q_hilo[:, o:o + S],
                          start=True, stop=False)
                if kt == 0:
                    pe.wait_ge(mrow_in[hh], 16 * n + 16)
                    if hh == 0:
                        pe.wait_ge(spread_b, 32 * n + 32)
                pe.matmul(st_bank(kt)[:, :],
                          k_lo[:, bass.ds(((n & (PAIRS - 1)) * 2 + hh) * S + kt * P, P)],
                          q_ext[:, o:o + S], start=False, stop=True).then_inc(scores_done, 1)

            def turn_tops(n, hh):
                pe.wait_ge(top_done, 8 * n + 4 * hh + 4)
                if hh == 0:
                    if not is_at(n, 0):
                        pe.wait_ge(mrow_done, 2 * n)
                elif not isinstance(n, int) or n > 1:
                    pe.wait_ge(ctx_out, n - 1)
                else:
                    pe.wait_ge(mrow_done, 2 * n + 1)
                pe.transpose(TURN[0:TPB, 0:P], row_max[:, hh * TPB:hh * TPB + TPB], ident[:, :]).then_inc(topT_done, 1)

            def attend(n, ring, hh):
                pe.wait_ge(lo_dve, (2 * n + hh + 1) * len(DVE_LO))
                pe.wait_ge(lo_pool, (2 * n + hh + 1) * len(POOL_LO))
                pe.wait_ge(qkv_lo, 3 * n + 3)
                if not (is_at(n, 0) and hh == 0):
                    pe.wait_ge(norm_done, 2 * n + hh)
                for t in range(TPB):
                    o = t * (DK + 1)
                    for kt in range(TPB):
                        a = (ring * TPB + kt) * 2 + hh
                        vh, vl = v_hi[:, a * VP:a * VP + DK + 1], v_lo[:, a * DK:a * DK + DK]
                        pcol = (hh * TPB + kt) * S + t * P
                        p_hi = probs[:, pcol:pcol + P].bitcast(BF16)[:, 1:2 * P:2]
                        pe.matmul(PV[:, o:o + DK + 1], p_hi, vh, start=kt == 0, stop=False)
                        pe.matmul(PV[:, o:o + DK], p_hi, vl, start=False, stop=False)
                        mm = pe.matmul(PV[:, o:o + DK + 1], probs_lo[:, pcol:pcol + P], vh, start=False,
                                       stop=kt == TPB - 1)
                mm.then_inc(pv_done, 1)

            def turn_context(n):
                pe.wait_ge(norm_done, 2 * n + 2)
                if is_at(n, ITERS - 1):
                    pe.wait_ge(ctx_out, ITERS - 1)
                elif is_at(n, ITERS - 2):
                    pe.wait_ge(mrow_done, 2 * ITERS)
                else:
                    pe.wait_ge(mrow_done, 2 * n + 5)
                for t in range(TPB):
                    mm = pe.transpose(TURN[:, t * P:t * P + P], ctx_n[:, t * P:t * P + P], ident[:, :])
                mm.then_inc(ctxT_done, 1)

            def out_product(n, odd):
                g = n & (PAIRS - 1)
                c_hi = ctxT[:, :].bitcast(BF16)[:, 1:2 * S:2]
                pe.wait_ge(ctx_lo, n + 1)
                if not odd:
                    pe.wait_ge(wout_read, (n >> 1) + 1)
                pe.matmul(WOUT[:, :], w_hi[:, bass.ds(WO + g * P, P)], c_hi, start=not odd, stop=False)
                pe.matmul(WOUT[:, :], w_lo[:, bass.ds(WO + g * P, P)], c_hi, start=False, stop=False)
                pe.matmul(WOUT[:, :], w_hi[:, bass.ds(WO + g * P, P)], ctxT_lo[:, :], start=False,
                          stop=odd).then_inc(wo_done, 1)

            def iteration(it, i):
                ring, nxt, nring = i % RING, it + 1, (i + 1) % RING
                after, last = not is_at(it, 0), is_at(it, ITERS - 1)
                project, rate = not last and not is_at(it, ITERS - 2), not last
                scores(it, ring, 0, 0)
                scores(it, ring, 0, 1)
                rough_scores(it, ring, 1, 2)
                rough_scores(it, ring, 1, 3)
                if project:
                    q_or_k(it + 2, WQ, 0)
                scores(it, ring, 0, 2)
                scores(it, ring, 0, 3)
                turn_tops(it, 1)
                if rate:
                    rough_scores(nxt, nring, 0, 0)
                    rough_scores(nxt, nring, 0, 1)
                if after:
                    attend(it - 1, (i - 1) % RING, 1)
                if project:
                    q_or_k(it + 2, WK, 1)
                if after and not is_at(it, 1):
                    out_product(it - 2, odd=i % 2 == 1)
                scores(it, ring, 1, 0)
                scores(it, ring, 1, 1)
                if rate:
                    rough_scores(nxt, nring, 0, 2)
                    rough_scores(nxt, nring, 0, 3)
                scores(it, ring, 1, 2)
                scores(it, ring, 1, 3)
                if rate:
                    turn_tops(nxt, 0)
                    rough_scores(nxt, nring, 1, 0)
                    rough_scores(nxt, nring, 1, 1)
                attend(it, ring, 0)
                if project:
                    v_proj(it + 2)
                if after:
                    turn_context(it - 1)

            pe.wait_ge(ln[0]["lo"], B)
            pe.wait_ge(w_lo_done, ATTN_PIECES)
            pe.wait_ge(setup_dve, 8)
            q_or_k(0, WQ, 0)
            q_or_k(0, WK, 1)
            v_proj(0)
            for t in range(TPB):
                rough_scores(0, 0, 0, t)
            pe.wait_ge(setup_act, 3)
            turn_tops(0, 0)
            q_or_k(1, WQ, 0)
            q_or_k(1, WK, 1)
            v_proj(1)
            rough_scores(0, 0, 1, 0)
            rough_scores(0, 0, 1, 1)
            pe.wait_ge(far_in, 16 * 2 * RING)
            pe.wait_ge(far_rows, 1)
            attention(pe, iteration)
            out_product(ITERS - 2, odd=False)
            attend(ITERS - 1, (ITERS - 1) % RING, 1)
            turn_context(ITERS - 1)
            out_product(ITERS - 1, odd=True)

            pe.wait_ge(summed, ITERS // 2 + 1)
            for b in range(B):
                if b >= 2:
                    pe.wait_ge(resid, b - 1)
                for t in range(TPB):
                    o = b * S + t * P
                    mm = pe.transpose(bank[2 + b % 2][:, t * P:t * P + P], attn_T[:, o:o + P], ident[:, :])
                mm.then_inc(attn_back, 1)
            layernorm(1)

            def up(b, c):
                e = (2, 0, 1)[c // HC]
                w = W1 + e * HID + (c % HC) * P
                if e == 2:
                    x_hi, x_lo = hT_hi[:, bass.ds(b * S, S)], hT_lo[:, bass.ds(b * S, S)]
                else:
                    x_hi, x_lo = xm[:, 2 * e * S:2 * e * S + S], xm[:, (2 * e + 1) * S:(2 * e + 2) * S]
                    if c % HC == 0:
                        pe.wait_ge(masked, 4 * b + 2 * e + 2)
                hb = bank[c % 2]
                if c >= 2:
                    pe.wait_ge(hid_done, CHUNKS * b + c - 1)
                else:
                    pe.wait_ge(hid_done, CHUNKS * b)
                pe.matmul(hb[:, :], w_hi[:, w:w + P], x_hi, start=True, stop=False)
                pe.matmul(hb[:, :], w_lo[:, w:w + P], x_hi, start=False, stop=False)
                pe.matmul(hb[:, :], w_hi[:, w:w + P], x_lo, start=False, stop=True).then_inc(up_done, 1)

            def down(b, c):
                e = (2, 0, 1)[c // HC]
                w = W2 + (e * HC + c % HC) * D
                o = (c % 4) * S
                h_hi = hid[:, o:o + S].bitcast(BF16)[:, 1:2 * S:2]
                pe.wait_ge(hid_lo_done, CHUNKS * b + c + 1)
                if c == 0:
                    pe.wait_ge(moe_done, b)
                pe.matmul(bank[2][:, :], w_hi[:, w:w + P], h_hi, start=c == 0, stop=False)
                pe.matmul(bank[2][:, :], w_lo[:, w:w + P], h_hi, start=False, stop=False)
                pe.matmul(bank[2][:, :], w_hi[:, w:w + P], hid_lo[:, o:o + S], start=False,
                          stop=c == CHUNKS - 1).then_inc(down_done, 1)

            pe.wait_ge(ln[1]["lo"], B)
            pe.wait_ge(w_lo_done, len(w_pieces))
            pe.wait_ge(setup_dve, 13)
            with pe.Fori(0, B) as b:
                pe.wait_ge(masked, 4 * b)
                for e in range(2):
                    g_hi, g_lo = gate_hi[:, e * P:e * P + P], gate_lo[:, e * P:e * P + P]
                    h_hi, h_lo = hT_hi[:, bass.ds(b * S, S)], hT_lo[:, bass.ds(b * S, S)]
                    pe.matmul(bank[3][:, :], g_hi, h_hi, start=e == 0, stop=False)
                    pe.matmul(bank[3][:, :], g_lo, h_hi, start=False, stop=False)
                    mm = pe.matmul(bank[3][:, :], g_hi, h_lo, start=False, stop=e == 1)
                mm.then_inc(gate_done, 1)
                for c in range(CHUNKS + 2):
                    if c < CHUNKS:
                        up(b, c)
                    if c >= 2:
                        down(b, c - 2)
                pe.wait_ge(moe_done, b + 1)
                pe.wait_ge(y_done, b)
                for t in range(TPB):
                    mm = pe.transpose(bank[4][:, t * P:t * P + P], moe_T[:, t * P:t * P + P], ident[:, :])
                mm.then_inc(moe_back, 1)


_INS = ['L0_attn_x', 'L0_attn_Wq', 'L0_attn_Wk', 'L0_attn_Wv', 'L0_attn_Wo', 'L0_attn_rel_emb', 'L0_ffn_gate_w',
        'L0_ffn_w1', 'L0_ffn_b1', 'L0_ffn_w2', 'L0_ffn_b2', 'L0_ffn_sw1', 'L0_ffn_sb1', 'L0_ffn_sw2', 'L0_ffn_sb2',
        'L0_c', 'L0_wmod']


def kernel(**inputs):
    import concourse.bacc as bacc
    from concourse.bass_utils import run_bass_kernel_spmd

    nc = bacc.Bacc("TRN2", target_bir_lowering=False, num_devices=1)
    arrays, ins, consts = {}, {}, {}
    for name in _INS:
        a = np.ascontiguousarray(inputs[name])
        arrays[f"in_{name}"] = a
        ins[name] = nc.dram_tensor(f"in_{name}", a.shape, mybir.dt.from_np(a.dtype), kind="ExternalInput").ap()
    for name, a in shape_constants().items():
        arrays[f"const_{name}"] = a
        consts[name] = nc.dram_tensor(f"const_{name}", a.shape, mybir.dt.from_np(a.dtype), kind="ExternalInput").ap()
    out = nc.dram_tensor("out_y", (B, S, D), F32, kind="ExternalOutput").ap()
    adaln_program(nc, ins, consts, out)
    r = run_bass_kernel_spmd(nc, [arrays], core_ids=[0])
    return r.results[0]["out_y"]
```

```python
from contextlib import ExitStack

import numpy as np

import concourse.bass as bass
from concourse import mybir

F32 = mybir.dt.float32
F16 = mybir.dt.float16
BF16 = mybir.dt.bfloat16
ALU = mybir.AluOpType
ACT = mybir.ActivationFunctionType
AXX = mybir.AxisListType.X

P = 128
B, S, D = 8, 512, 128
H, DK = 16, 64
TPB = S // P
TILES = B * TPB
PAIRS = H // 2
ITERS = B * PAIRS
RING = 3
UNROLL = 6
LOOPS = (ITERS - 4) // UNROLL
HID, EXPERTS = 512, 3
HC = HID // P
CHUNKS = EXPERTS * HC
EPS = 1e-5
BUCKETS, EXACT = 32, 8
FAR = 91
BAND = 2 * FAR + P - 2
OFFS = 2 * (FAR + P - 2) + 1
M_ROW = DK
M_SCALE = 32.0
FAR_ROW = M_ROW + 1

WQ, WK, WV, WO = 0, 1024, 2048, 3072
W1 = 4096
W2 = W1 + EXPERTS * HID
WCOLS = W2 + EXPERTS * HC * D

POOL_LO = (3,)
DVE_LO = (0, 1, 2)


def band_of(kt):
    first = P * kt - FAR + 1
    q0, q1 = max(0, first), min(S, first + BAND)
    return q0, q1, q0 - first


def bucket_of(n):
    a = abs(n)
    b = a if a < EXACT else EXACT + sum(a * a >= 64 * 2 ** j for j in range(1, EXACT))
    return b + (BUCKETS // 2 if n < 0 else 0)


def shape_constants():
    onehot = np.zeros((BUCKETS, OFFS), np.float32)
    for m in range(OFFS):
        onehot[bucket_of(m - OFFS // 2), m] = 1
    select = np.zeros((BUCKETS, P), np.float32)
    rowmask = np.zeros((P, 3 + TPB), np.float32)
    indicator = np.zeros((P, S), np.float16)
    rowmask[M_ROW, 2] = M_SCALE
    rowmask[M_ROW, 3:] = 1
    q = np.arange(S)
    for j in range(TPB):
        for side in range(2):
            for part in range(2):
                r = FAR_ROW + 4 * j + 2 * side + part
                select[bucket_of(-FAR if side == 0 else FAR), r] = 1
                rowmask[r, part] = 1
                rowmask[r, 3 + j] = 1
                indicator[r] = (q <= P * j - FAR) if side == 0 else (q >= P * j + P - 1 + FAR)
    return {"ident": np.eye(P, dtype=np.float32), "onehot": onehot, "select": select,
            "rowmask": rowmask, "indicator": indicator}


def adaln_program(nc, ins, consts, out):
    x_d = ins["L0_attn_x"].rearrange("b s d -> (b s) d").rearrange("(t p) d -> p t d", p=P)
    out_d = out.rearrange("b s d -> (b s) d").rearrange("(t p) d -> p t d", p=P)
    bias_scratch = nc.dram_tensor("bias_scratch", (P, H, OFFS), F32, kind="Internal").ap()

    ctx = ExitStack()
    with ctx:
        ctx.enter_context(nc.allow_non_contiguous_dma(reason="small transposed vectors"))

        def sb(name, shape, dt=F32):
            return ctx.enter_context(nc.sbuf_tensor(name, shape, dt))

        def sem(name):
            return ctx.enter_context(nc.semaphore(name))

        bank = [ctx.enter_context(nc.psum_tensor(f"bank{i}", [P, 512], F32)) for i in range(8)]

        x = sb("x", [P, TILES * D])
        hT_hi = sb("hT_hi", [P, B * S], F16)
        hT_lo = sb("hT_lo", [P, B * S], F16)
        w_raw = sb("w_raw", [P, WCOLS])
        w_hi = sb("w_hi", [P, WCOLS], F16)
        w_lo = sb("w_lo", [P, WCOLS], F16)
        attn_T = w_raw[:, 0:B * S]
        k_lo = sb("k_lo", [P, H * S], F16)
        exp_bias = sb("exp_bias", [P, H * BAND])
        pair_hi = sb("pair_hi", [P, 2 * S], F16)
        pair_lo = sb("pair_lo", [P, 2 * S], F16)
        q_hilo = sb("q_hilo", [P, RING * 2 * S], F16)
        q_ext = sb("q_ext", [P, RING * 2 * S], F16)
        k_hihi = sb("k_hihi", [P, RING * 2 * S], F16)
        VP = DK + 2
        v_hi = sb("v_hi", [P, RING * 2 * TPB * VP], F16)
        v_lo = sb("v_lo", [P, RING * 2 * TPB * DK], F16)
        probs = sb("probs", [P, 2 * TPB * S])
        probs_lo = sb("probs_lo", [P, 2 * TPB * S], F16)
        row_max = sb("row_max", [P, 2 * TPB])
        max_row = sb("max_row", [TPB, 2 * P], F16)
        recip = sb("recip", [P, TPB])
        ctx_n = sb("ctx_n", [P, TPB * P])
        ctxT = sb("ctxT", [P, S])
        ctxT_lo = sb("ctxT_lo", [P, S], F16)
        attn_part = sb("attn_part", [P, S])
        ident = sb("ident_sb", [P, P])
        onehot = sb("onehot_sb", [BUCKETS, OFFS])
        select = sb("select_sb", [BUCKETS, P])
        rowmask = sb("rowmask_sb", [P, 3 + TPB])
        rel = sb("rel", [BUCKETS, H])
        rel_all = sb("rel_all", [P, BUCKETS * H])
        relT = sb("relT", [H, BUCKETS])
        rel_top = sb("rel_top", [P, H])
        relT_ntop = sb("relT_ntop", [H, 1])
        eb_row = sb("eb_row", [H, OFFS])
        far = sb("far", [P, 3 * H])
        far_hi = sb("far_hi", [P, H], F16)
        far_tile = sb("far_tile", [P, H * TPB])
        cT = sb("cT", [P, 3 * B])
        wmod = sb("wmod", [P, 6 * D])
        mod = sb("mod", [P, 6 * B])
        gates = sb("gates", [P, 2 * 4 * B])
        b1T = sb("b1T", [P, CHUNKS])
        b2T = sb("b2T", [P, EXPERTS + 2])
        b2g = sb("b2g", [P, B])
        gateT = sb("gateT", [P, 2])
        ones = sb("ones", [P, P])
        gate_hi = sb("gate_hi", [P, 2 * P], F16)
        gate_lo = sb("gate_lo", [P, 2 * P], F16)
        stats = sb("stats", [P, TILES * 6])
        mean_var = sb("mean_var", [P, TILES * 2])
        var_eps = sb("var_eps", [P, TILES])
        minus_half = sb("minus_half", [P, TILES])
        rstd = sb("rstd", [P, TILES])
        xn = [probs[:, 0:2 * S], pair_hi[:, :].bitcast(F32)]
        h32 = [probs[:, 2 * S:4 * S], pair_lo[:, :].bitcast(F32)]
        hid = probs[:, 0:4 * S]
        hid_lo = probs_lo[:, 0:4 * S]
        xm = probs_lo[:, 4 * S:8 * S]
        moe_T = ctx_n
        back_T = ctxT

        def mod_col(i, b):
            return mod[:, bass.ds(i * B + b, 1)]

        (consts_in, x_in, small_in, attn_w_in, ffn_w_in, wmod_in, bias_out, bias_in, far_in, spread_a, spread_b,
         stored) = map(sem, ("consts_in", "x_in", "small_in", "attn_w_in", "ffn_w_in", "wmod_in", "bias_out",
                             "bias_in", "far_in", "spread_a", "spread_b", "stored"))
        mrow_in = [sem("mrow_in0"), sem("mrow_in1")]
        setup_dve = sem("setup_dve")
        setup_act = sem("setup_act")
        setup_pe = sem("setup_pe")
        w_hi_done, w_lo_done = sem("w_hi_done"), sem("w_lo_done")
        fills = sem("fills")
        far_rows = sem("far_rows")
        ln = [{k: sem(f"ln{ph}_{k}") for k in ("stats", "aggr", "eps", "rstd", "xn", "xT", "h32", "hi", "lo")}
              for ph in range(2)]
        (proj_done, scores_done, tops_done, top_done, topT_done, mrow_done, qkv_hi, qkv_lo, exp_done, band_done,
         lo_dve, lo_pool, pv_done, recip_done, norm_done, ctxT_done, ctx_out, ctx_lo, wo_done, wout_read,
         summed) = map(sem, ("proj_done", "scores_done", "tops_done", "top_done", "topT_done", "mrow_done", "qkv_hi",
                             "qkv_lo", "exp_done", "band_done", "lo_dve", "lo_pool", "pv_done", "recip_done",
                             "norm_done", "ctxT_done", "ctx_out", "ctx_lo", "wo_done", "wout_read", "summed"))
        back_in, attn_back, resid = sem("back_in"), sem("attn_back"), sem("resid")
        (gate_done, masked, up_done, hid_done, hid_lo_done, down_done, moe_done, moe_back, y_done) = map(
            sem, ("gate_done", "masked", "up_done", "hid_done", "hid_lo_done", "down_done", "moe_done", "moe_back",
                  "y_done"))

        block = ctx.enter_context(nc.Block())

        def st_bank(kt):
            return bank[kt % 2]
        def s_bank(t):
            return bank[2 + t % 2]
        PV, PROJ, TURN, WOUT = bank[4], bank[5], bank[6], bank[7]

        def slot(ring, hh):
            return (2 * ring + hh) * S

        def attention(eng, iteration):
            iteration(0, 0)
            iteration(1, 1)
            with eng.Fori(0, LOOPS) as j:
                for u in range(UNROLL):
                    iteration(UNROLL * j + 2 + u, 2 + u)
            iteration(ITERS - 2, ITERS - 2)
            iteration(ITERS - 1, ITERS - 1)

        def batches(eng, experts):
            experts(0, 0)
            with eng.Fori(0, B // 2 - 1) as j:
                for u in range(2):
                    experts(2 * j + 1 + u, (1 + u) % 2)
            experts(B - 1, 1)

        def is_at(it, n):
            return isinstance(it, int) and it == n

        w_pieces = [
            (WQ, 1024, ins["L0_attn_Wq"]), (WK, 1024, ins["L0_attn_Wk"]), (WV, 1024, ins["L0_attn_Wv"]),
            (WO, 1024, ins["L0_attn_Wo"].rearrange("(g p) n -> p g n", p=P)),
            (W1, 1024, ins["L0_ffn_w1"].rearrange("e d h -> d e h")),
            (W1 + 1024, 512, ins["L0_ffn_sw1"]),
            (W2, 1024, ins["L0_ffn_w2"].rearrange("e (c p) d -> p (e c) d", p=P)),
            (W2 + 1024, 512, ins["L0_ffn_sw2"].rearrange("(c p) d -> p c d", p=P)),
        ]
        ATTN_PIECES = 4

        def w_part(t, o, n):
            if o in (WQ, WK):
                return t[:, o:o + n].rearrange("p (g d h) -> p g h d", h=2, d=DK)
            return t[:, o:o + n]

        def w_source(o, n):
            if o in (WQ, WK):
                return w_raw[:, o:o + n].rearrange("p (g h d) -> p g h d", h=2, d=DK)
            return w_raw[:, o:o + n]

        def w_view(o, n, src):
            t = w_raw[:, o:o + n]
            return t if len(src.shape) == 2 else t.rearrange("p (g n) -> p g n", n=src.shape[-1])

        @block.sync
        def _(sp):
            sp.dma_start(x[:, :].rearrange("p (t d) -> p t d", d=D), x_d).then_inc(x_in, 16)
            for o, n, src in w_pieces[:ATTN_PIECES]:
                sp.dma_start(w_view(o, n, src), src).then_inc(attn_w_in, 16)
            for o, n, src in w_pieces[ATTN_PIECES:]:
                sp.dma_start(w_view(o, n, src), src).then_inc(ffn_w_in, 16)
            sp.wait_ge(setup_act, 3)
            sp.dma_start(bias_scratch.rearrange("p h m -> h p m"),
                         eb_row[:, :].unsqueeze(1).to_broadcast([H, P, OFFS])).then_inc(bias_out, 16)
            sp.wait_ge(bias_out, 16)
            toeplitz = bass.AP(tensor=bias_scratch.tensor, offset=bias_scratch.offset + P - 1,
                               ap=[[H * OFFS - 1, P], [OFFS, H], [1, BAND]])
            sp.dma_start(exp_bias[:, :].rearrange("p (h c) -> p h c", h=H), toeplitz).then_inc(bias_in, 16)

            def max_row_in(n, ring, hh):
                sp.wait_ge(mrow_done, 2 * n + hh + 1)
                o = slot(ring, hh)
                sp.dma_start(q_ext[M_ROW:M_ROW + 1, o:o + S].rearrange("o (t c) -> o t c", c=P),
                             max_row[:, hh * P:hh * P + P]).then_inc(mrow_in[hh], 16)

            def spread(dst, src, done):
                sp.dma_start(dst.rearrange("p (h c) -> p h c", h=2), src).then_inc(done, 16)

            def spread_q(n, ring):
                o = slot(ring, 0)
                sp.wait_ge(qkv_hi, 3 * n + 1)
                spread(q_hilo[0:DK, o:o + 2 * S], pair_hi[:, 0:S], spread_a)
                spread(q_ext[0:DK, o:o + 2 * S], pair_hi[:, 0:S], spread_b)
                sp.wait_ge(qkv_lo, 3 * n + 1)
                spread(q_hilo[DK:P, o:o + 2 * S], pair_lo[:, 0:S], spread_a)

            def spread_k(n, ring):
                o = slot(ring, 0)
                sp.wait_ge(qkv_hi, 3 * n + 2)
                spread(k_hihi[0:DK, o:o + 2 * S], pair_hi[:, S:2 * S], spread_a)
                spread(k_hihi[DK:P, o:o + 2 * S], pair_hi[:, S:2 * S], spread_a)
                sp.wait_ge(qkv_lo, 3 * n + 2)
                at = (((n + PAIRS) << 1) & (2 * PAIRS - 2)) << 9
                spread(k_lo[0:DK, bass.ds(at, 2 * S)], pair_lo[:, S:2 * S], spread_b)

            def iteration(it, i):
                max_row_in(it, i % RING, 1)
                if not is_at(it, ITERS - 2) and not is_at(it, ITERS - 1):
                    spread_q(it + 2, (i + 2) % RING)
                    spread_k(it + 2, (i + 2) % RING)
                if not is_at(it, ITERS - 1):
                    max_row_in(it + 1, (i + 1) % RING, 0)

            sp.wait_ge(far_in, 16 * 2 * RING)
            spread_q(0, 0)
            spread_k(0, 0)
            max_row_in(0, 0, 0)
            spread_q(1, 1)
            spread_k(1, 1)
            attention(sp, iteration)

            with sp.Fori(0, B) as b:
                sp.wait_ge(y_done, b + 1)
                sp.dma_start(out_d[:, bass.ds(b * TPB, TPB), :],
                             x[:, bass.ds(b * S, S)].rearrange("p (t d) -> p t d", d=D)).then_inc(stored, 16)
            sp.wait_ge(stored, 16 * B)

        @block.gpsimd
        def _(pool):
            pool.dma_start(cT[:, 0:B], ins["L0_c"].rearrange("b d -> d b")).then_inc(small_in, 16)
            pool.dma_start(rel[:, :], ins["L0_attn_rel_emb"]).then_inc(small_in, 16)
            pool.dma_start(relT[:, :], ins["L0_attn_rel_emb"].rearrange("n h -> h n")).then_inc(small_in, 16)
            pool.dma_start(rel_all[:, :].rearrange("p (n h) -> p n h", h=H),
                           bass.AP(tensor=ins["L0_attn_rel_emb"].tensor, offset=ins["L0_attn_rel_emb"].offset,
                                   ap=[[0, P], [H, BUCKETS], [1, H]])).then_inc(small_in, 16)
            pool.dma_start(wmod[:, :], ins["L0_wmod"]).then_inc(wmod_in, 16)
            pool.dma_start(b1T[:, 0:2 * HC].rearrange("p (e c) -> p e c", e=2),
                           ins["L0_ffn_b1"].rearrange("e (c p) -> p e c", p=P)).then_inc(small_in, 16)
            pool.dma_start(b1T[:, 2 * HC:3 * HC],
                           ins["L0_ffn_sb1"].rearrange("(c p) -> p c", p=P)).then_inc(small_in, 16)
            pool.dma_start(b2T[:, 0:2], ins["L0_ffn_b2"].rearrange("e p -> p e")).then_inc(small_in, 16)
            pool.dma_start(b2T[:, 2:3], ins["L0_ffn_sb2"].rearrange("(p o) -> p o", o=1)).then_inc(small_in, 16)
            pool.dma_start(gateT[:, :], ins["L0_ffn_gate_w"].rearrange("e p -> p e")).then_inc(small_in, 16)
            pool.memset(minus_half[:, :], -0.5).then_inc(fills, 1)
            pool.memset(v_hi[:, :], 1.0).then_inc(fills, 1)
            pool.memset(ones[:, :], 1.0).then_inc(fills, 1)

            def layernorm():
                s = ln[0]
                pool.wait_ge(s["eps"], 1)
                pool.tensor_tensor(rstd[:, :], var_eps[:, :], minus_half[:, :], ALU.pow).then_inc(s["rstd"], 1)
                with pool.Fori(0, B // 2) as j:
                    for par in range(2):
                        b = 2 * j + par
                        pool.wait_ge(s["hi"], b + 1)
                        pool.tensor_tensor(hT_lo[:, bass.ds(b * S, S)], h32[0][:, par * S:par * S + S],
                                           hT_hi[:, bass.ds(b * S, S)], ALU.subtract).then_inc(s["lo"], 1)

            def second_rstd(b, par):
                s = ln[1]
                o = par * TPB
                pool.wait_ge(s["eps"], b + 1)
                pool.tensor_tensor(rstd[:, o:o + TPB], var_eps[:, o:o + TPB], minus_half[:, 0:TPB],
                                   ALU.pow).then_inc(s["rstd"], 1)

            def second_lo(b):
                s = ln[1]
                pool.wait_ge(s["hi"], b + 1)
                at = bass.ds(b * S, S)
                pool.tensor_tensor(hT_lo[:, at], h32[1][:, :], hT_hi[:, at], ALU.subtract).then_inc(s["lo"], 1)

            pool.wait_ge(fills, 1)
            layernorm()
            pool.wait_ge(w_lo_done, len(w_pieces))
            pool.memset(attn_T, 0.0).then_inc(summed, 1)
            pool.wait_ge(bias_in, 16)

            def numerators(n, hh):
                g2 = ((n & (PAIRS - 1)) * 2 + hh) * BAND
                for kt in range(TPB):
                    q0, q1, c0 = band_of(kt)
                    o = (hh * TPB + kt) * S
                    pool.wait_ge(exp_done, 8 * n + 4 * hh + kt + 1)
                    at = ((g2 << kt) >> kt) + c0
                    pool.tensor_tensor(probs[:, o + q0:o + q1], probs[:, o + q0:o + q1],
                                       exp_bias[:, bass.ds(at, q1 - q0)], ALU.mult).then_inc(band_done, 1)
                    if kt in POOL_LO:
                        pool.wait_ge(band_done, 8 * n + 4 * hh + kt + 1)
                        pool.tensor_tensor(probs_lo[:, o:o + S], probs[:, o:o + S],
                                           probs[:, o:o + S].bitcast(BF16)[:, 1:2 * S:2],
                                           ALU.subtract).then_inc(lo_pool, 1)

            def context_lo(n):
                pool.wait_ge(ctx_out, n + 1)
                pool.tensor_tensor(ctxT_lo[:, :], ctxT[:, :], ctxT[:, :].bitcast(BF16)[:, 1:2 * S:2],
                                   ALU.subtract).then_inc(ctx_lo, 1)

            def add_pairs(m):
                y = attn_T[:, bass.ds(((m >> 2) & (B - 1)) * S, S)]
                pool.wait_ge(wout_read, m + 2)
                pool.wait_ge(summed, m + 1)
                pool.tensor_tensor(y, y, attn_part[:, :], ALU.add).then_inc(summed, 1)

            def iteration(it, i):
                if not is_at(it, 0) and not is_at(it, 1):
                    context_lo(it - 2)
                numerators(it, 0)
                if is_at(it, ITERS - 1):
                    second_rstd(0, 0)
                numerators(it, 1)
                if is_at(it, ITERS - 1):
                    second_lo(0)
                    context_lo(it - 1)
                if i % 2 == 1 and not is_at(it, 1):
                    add_pairs(it // 2 - 1 if isinstance(it, int) else (it >> 1) - 1)

            attention(pool, iteration)
            context_lo(ITERS - 1)
            add_pairs(ITERS // 2 - 1)

            def experts(b, par):
                if not is_at(b, B - 1):
                    second_rstd(b + 1, 1 - par)
                    second_lo(b + 1)

            batches(pool, experts)

        @block.scalar
        def _(act):
            act.dma_start(ident[:, :], consts["ident"]).then_inc(consts_in, 16)
            act.dma_start(onehot[:, :], consts["onehot"]).then_inc(consts_in, 16)
            act.dma_start(select[:, :], consts["select"]).then_inc(consts_in, 16)
            act.dma_start(rowmask[:, :], consts["rowmask"]).then_inc(consts_in, 16)
            for s in range(2 * RING):
                act.dma_start(q_ext[DK:P, s * S:s * S + S], consts["indicator"][DK:P, :]).then_inc(far_in, 16)

            act.wait_ge(small_in, 16 * 9)
            act.activation(cT[:, B:2 * B], cT[:, 0:B], ACT.Exp, scale=-1.0).then_inc(setup_act, 1)
            act.wait_ge(setup_pe, 1)
            act.activation(mod[:, :], PROJ[:, 0:6 * B], ACT.Copy).then_inc(setup_act, 1)
            act.wait_ge(setup_pe, 2)
            act.wait_ge(setup_dve, 4)
            act.activation(eb_row[:, :], TURN[0:H, 0:OFFS], ACT.Exp, bias=relT_ntop[:, 0:1]).then_inc(setup_act, 1)

            def layernorm():
                s = ln[0]
                with act.Fori(0, B // 2) as j:
                    for par in range(2):
                        b = 2 * j + par
                        act.wait_ge(s["xT"], b + 1)
                        act.wait_ge(s["lo"], 2 * j)
                        act.activation(h32[0][:, par * S:par * S + S], bank[par][:, :], ACT.Identity,
                                       bias=mod_col(0, b), scale=mod_col(1, b)).then_inc(s["h32"], 1)
                        act.wait_ge(s["h32"], b + 1)
                        act.activation(hT_hi[:, bass.ds(b * S, S)], h32[0][:, par * S:par * S + S],
                                       ACT.Copy).then_inc(s["hi"], 1)

            def modulate(b):
                s = ln[1]
                act.wait_ge(s["xT"], b + 1)
                if not is_at(b, 0):
                    act.wait_ge(s["lo"], b)
                act.activation(h32[1][:, :], PROJ[:, :], ACT.Identity,
                               bias=mod_col(3, b), scale=mod_col(4, b)).then_inc(s["h32"], 1)

            def modulated_hi(b):
                s = ln[1]
                act.wait_ge(s["h32"], b + 1)
                act.activation(hT_hi[:, bass.ds(b * S, S)], h32[1][:, :], ACT.Copy).then_inc(s["hi"], 1)

            def back_copy(b):
                act.wait_ge(summed, 1 + (b + 1) * (PAIRS // 2))
                if is_at(b, 1):
                    act.wait_ge(wo_done, ITERS)
                else:
                    act.wait_ge(attn_back, b)
                act.activation(back_T[:, :], attn_T[:, bass.ds(b * S, S)], ACT.Copy).then_inc(back_in, 1)

            act.wait_ge(attn_w_in, 16 * ATTN_PIECES)
            for o, n, _ in w_pieces[:ATTN_PIECES]:
                act.activation(w_part(w_hi, o, n), w_source(o, n), ACT.Copy).then_inc(w_hi_done, 1)
            act.wait_ge(setup_dve, 7)
            layernorm()
            act.wait_ge(ffn_w_in, 16 * (len(w_pieces) - ATTN_PIECES))
            for o, n, _ in w_pieces[ATTN_PIECES:]:
                act.activation(w_part(w_hi, o, n), w_source(o, n), ACT.Copy).then_inc(w_hi_done, 1)
            act.wait_ge(setup_dve, 12)
            act.activation(k_lo[DK:P, :].rearrange("p (a c) -> p a c", c=P),
                           far_tile[DK:P, :].unsqueeze(2).to_broadcast([DK, H * TPB, P]),
                           ACT.Copy).then_inc(far_rows, 1)

            def exponentials(n, hh, kts):
                for kt in kts:
                    if kt == 0 and not (isinstance(n, int) and n == 0):
                        act.wait_ge(pv_done, 2 * n - 1 + hh)
                    o = (hh * TPB + kt) * S
                    act.wait_ge(scores_done, 8 * n + 4 * hh + kt + 1)
                    act.activation(probs[:, o:o + S], st_bank(kt)[:, :], ACT.Exp).then_inc(exp_done, 1)

            def pair_hi_part(n, k):
                act.wait_ge(proj_done, 3 * n + k + 1)
                if not (isinstance(n, int) and n == 0):
                    act.wait_ge(spread_a, 64 * n)
                    act.wait_ge(spread_b, 32 * n)
                act.activation(pair_hi[:, k * S:k * S + S], PROJ[:, :], ACT.Copy).then_inc(qkv_hi, 1)

            def v_hi_part(n, ring):
                act.wait_ge(proj_done, 3 * n + 3)
                o = ring * 2 * TPB * VP
                act.activation(v_hi[:, o:o + 2 * TPB * VP].rearrange("p (a c) -> p a c", c=VP)[:, :, 0:DK],
                               PROJ[:, :].rearrange("p (a c) -> p a c", c=DK), ACT.Copy).then_inc(qkv_hi, 1)

            def max_row_out(n, hh):
                act.wait_ge(topT_done, 2 * n + hh + 1)
                if not (isinstance(n, int) and n == 0):
                    act.wait_ge(mrow_in[hh], 16 * n)
                act.activation(max_row[:, hh * P:hh * P + P], TURN[0:TPB, 0:P], ACT.Copy,
                               scale=-1.0 / M_SCALE).then_inc(mrow_done, 1)

            def context_out(n):
                act.wait_ge(ctxT_done, n + 1)
                act.activation(ctxT[:, :], TURN[:, :], ACT.Copy).then_inc(ctx_out, 1)

            def attn_part_out(m):
                act.wait_ge(wo_done, 2 * m + 2)
                act.wait_ge(summed, m + 1)
                act.activation(attn_part[:, :], WOUT[:, :], ACT.Copy,
                               scale=gates[:, bass.ds((m >> 2) & (B - 1), 1)]).then_inc(wout_read, 1)

            def iteration(it, i):
                project, rate = not is_at(it, ITERS - 2) and not is_at(it, ITERS - 1), not is_at(it, ITERS - 1)
                exponentials(it, 0, (0, 1))
                if project:
                    pair_hi_part(it + 2, 0)
                exponentials(it, 0, (2, 3))
                max_row_out(it, 1)
                if project:
                    pair_hi_part(it + 2, 1)
                exponentials(it, 1, (0, 1))
                exponentials(it, 1, (2, 3))
                if i % 2 == 1 and not is_at(it, 1):
                    attn_part_out(it // 2 - 1 if isinstance(it, int) else (it >> 1) - 1)
                if rate:
                    max_row_out(it + 1, 0)
                else:
                    modulate(0)
                    modulated_hi(0)
                if project:
                    v_hi_part(it + 2, (i + 2) % RING)
                if not is_at(it, 0):
                    context_out(it - 1)

            pair_hi_part(0, 0)
            pair_hi_part(0, 1)
            v_hi_part(0, 0)
            max_row_out(0, 0)
            pair_hi_part(1, 0)
            pair_hi_part(1, 1)
            v_hi_part(1, 1)
            attention(act, iteration)

            def experts(b, par):
                for c in range(CHUNKS):
                    if c == 1 and is_at(b, 0):
                        context_out(ITERS - 1)
                    if c == 3 and is_at(b, 0):
                        attn_part_out(ITERS // 2 - 1)
                    if c == 3 and not is_at(b, B - 1):
                        back_copy(b + 1)
                    if c == 10 and not is_at(b, B - 1):
                        modulate(b + 1)
                    if c == 11 and not is_at(b, B - 1):
                        modulated_hi(b + 1)
                    e = (2, 0, 1)[c // HC]
                    act.wait_ge(up_done, CHUNKS * b + c + 1)
                    if c >= 4:
                        act.wait_ge(down_done, CHUNKS * b + c - 3)
                    elif is_at(b, 0):
                        act.wait_ge(pv_done, 2 * ITERS - 1)
                    else:
                        act.wait_ge(down_done, CHUNKS * b)
                    act.activation(hid[:, (c % 4) * S:(c % 4) * S + S], bank[c % 2][:, :], ACT.Relu,
                                   bias=b1T[:, e * HC + c % HC:e * HC + c % HC + 1]).then_inc(hid_done, 1)
                act.wait_ge(down_done, CHUNKS * b + CHUNKS)
                if not is_at(b, 0):
                    act.wait_ge(moe_back, b)
                act.activation(moe_T[:, :], bank[2][:, :], ACT.Identity, bias=b2g[:, bass.ds(b, 1)],
                               scale=gates[:, bass.ds(4 * B + b, 1)]).then_inc(moe_done, 1)

            batches(act, experts)

        @block.vector
        def _(dve):
            dve.wait_ge(small_in, 16 * 9)
            dve.reduce_max(rel_top[:, :], rel_all[:, :].rearrange("p (n h) -> p h n", h=H), AXX).then_inc(setup_dve, 1)
            dve.reduce_max(relT_ntop[:, :], relT[:, :], AXX).then_inc(setup_dve, 1)
            dve.wait_ge(setup_dve, 2)
            dve.tensor_scalar(relT_ntop[:, :], relT_ntop[:, :], -1.0, None, ALU.mult).then_inc(setup_dve, 1)
            dve.wait_ge(setup_act, 1)
            dve.tensor_scalar(cT[:, B:2 * B], cT[:, B:2 * B], 1.0, None, ALU.add).then_inc(setup_dve, 1)
            dve.wait_ge(setup_dve, 4)
            dve.reciprocal(cT[:, 2 * B:3 * B], cT[:, B:2 * B]).then_inc(setup_dve, 1)
            dve.wait_ge(setup_dve, 5)
            dve.tensor_tensor(cT[:, B:2 * B], cT[:, 0:B], cT[:, 2 * B:3 * B], ALU.mult).then_inc(setup_dve, 1)
            dve.wait_ge(setup_act, 2)
            dve.tensor_scalar(mod[:, B:2 * B], mod[:, B:2 * B], 1.0, None, ALU.add)
            dve.tensor_scalar(mod[:, 4 * B:5 * B], mod[:, 4 * B:5 * B], 1.0, None, ALU.add)
            for k, i in enumerate((2, 5)):
                raw = mod[:, i * B:i * B + B]
                o = k * 4 * B
                dve.tensor_scalar(gates[:, o + B:o + 2 * B], raw, -1.0, None, ALU.mult)
                dve.tensor_scalar(gates[:, o + 2 * B:o + 3 * B], raw, 0.0, 2.0, ALU.is_ge, ALU.mult)
                dve.drain()
                dve.tensor_tensor(gates[:, o + B:o + 2 * B], gates[:, o + B:o + 2 * B], raw, ALU.max)
                dve.tensor_scalar(gates[:, o + 2 * B:o + 3 * B], gates[:, o + 2 * B:o + 3 * B], -1.0, None, ALU.add)
                dve.drain()
                dve.tensor_scalar(gates[:, o + B:o + 2 * B], gates[:, o + B:o + 2 * B], 0.25, None, ALU.max)
                dve.drain()
                last = dve.tensor_tensor(gates[:, o:o + B], gates[:, o + B:o + 2 * B],
                                         gates[:, o + 2 * B:o + 3 * B], ALU.mult)
            last.then_inc(setup_dve, 1)

            def layernorm():
                s = ln[0]
                with dve.Fori(0, TILES // 8) as j:
                    for k in range(8):
                        dve.bn_stats(stats[:, bass.ds((8 * j + k) * 6, 6)],
                                     x[:, bass.ds((8 * j + k) * P, P)]).then_inc(s["stats"], 1)
                dve.wait_ge(s["stats"], TILES)
                for n in range(TILES):
                    dve.bn_aggr(mean_var[:, 2 * n:2 * n + 2], stats[:, 6 * n:6 * n + 6]).then_inc(s["aggr"], 1)
                dve.wait_ge(s["aggr"], TILES)
                dve.tensor_scalar(var_eps[:, :], mean_var[:, 1:2 * TILES:2], EPS, None, ALU.add).then_inc(s["eps"], 1)
                dve.wait_ge(s["rstd"], 1)
                with dve.Fori(0, B // 2) as j:
                    for par in range(2):
                        b = 2 * j + par
                        dve.wait_ge(s["xT"], 2 * j)
                        for t in range(TPB):
                            n = b * TPB + t
                            dve.tensor_scalar(xn[0][:, par * S + t * P:par * S + t * P + P],
                                              x[:, bass.ds(b * S + t * P, P)], mean_var[:, bass.ds(2 * n, 1)],
                                              rstd[:, bass.ds(n, 1)], ALU.subtract, ALU.mult).then_inc(s["xn"], 1)

            def add_attention(b):
                dve.wait_ge(attn_back, b + 1)
                xb = x[:, bass.ds(b * S, S)]
                dve.tensor_tensor(xb, xb, PROJ[:, :], ALU.add).then_inc(resid, 1)

            def row_stats(b, par):
                for t in range(TPB):
                    o = (par * TPB + t) * 6
                    dve.bn_stats(stats[:, o:o + 6], x[:, bass.ds(b * S + t * P, P)]).then_inc(ln[1]["stats"], 1)

            def variances(b, par):
                s = ln[1]
                for t in range(TPB):
                    n = par * TPB + t
                    dve.bn_aggr(mean_var[:, 2 * n:2 * n + 2], stats[:, 6 * n:6 * n + 6]).then_inc(s["aggr"], 1)
                dve.wait_ge(s["aggr"], (b + 1) * TPB)
                o = par * TPB
                dve.tensor_scalar(var_eps[:, o:o + TPB], mean_var[:, 2 * o + 1:2 * (o + TPB):2], EPS, None,
                                  ALU.add).then_inc(s["eps"], 1)

            def normalise_rows(b, par):
                dve.wait_ge(ln[1]["rstd"], b + 1)
                for t in range(TPB):
                    n = par * TPB + t
                    dve.tensor_scalar(xn[1][:, t * P:t * P + P], x[:, bass.ds(b * S + t * P, P)],
                                      mean_var[:, 2 * n:2 * n + 1], rstd[:, n:n + 1], ALU.subtract,
                                      ALU.mult).then_inc(ln[1]["xn"], 1)

            dve.wait_ge(x_in, 16)
            layernorm()
            for k, (o, n, _) in enumerate(w_pieces[:ATTN_PIECES]):
                dve.wait_ge(w_hi_done, k + 1)
                dve.tensor_tensor(w_part(w_lo, o, n), w_source(o, n), w_part(w_hi, o, n),
                                  ALU.subtract).then_inc(w_lo_done, 1)
            dve.wait_ge(setup_pe, 3)
            dve.wait_ge(consts_in, 16 * 4)
            dve.tensor_tensor(far[:, 0:H], WOUT[:, 0:H], rel_top[:, :], ALU.subtract).then_inc(setup_dve, 1)
            dve.wait_ge(setup_dve, 8)
            dve.tensor_copy(far_hi[:, :], far[:, 0:H]).then_inc(setup_dve, 1)
            dve.wait_ge(setup_dve, 9)
            dve.tensor_tensor(far[:, H:2 * H], far[:, 0:H], far_hi[:, :], ALU.subtract).then_inc(wout_read, 1)
            dve.tensor_scalar(far[:, 2 * H:3 * H], far_hi[:, :], rowmask[:, 0:1], rowmask[:, 2:3],
                              ALU.mult, ALU.add).then_inc(setup_dve, 1)
            dve.wait_ge(setup_dve, 10)
            dve.scalar_tensor_tensor(far[:, 0:H], far[:, H:2 * H], rowmask[:, 1:2], far[:, 2 * H:3 * H],
                                     ALU.mult, ALU.add).then_inc(setup_dve, 1)
            dve.wait_ge(setup_dve, 11)
            dve.tensor_tensor(far_tile[:, :].rearrange("p (h j) -> p h j", j=TPB),
                              far[:, 0:H].unsqueeze(2).to_broadcast([P, H, TPB]),
                              rowmask[:, 3:3 + TPB].unsqueeze(1).to_broadcast([P, H, TPB]),
                              ALU.mult).then_inc(setup_dve, 1)
            dve.wait_ge(fills, 3)
            for e in range(2):
                sign = -1.0 if e == 0 else 1.0
                dve.tensor_scalar(ctx_n[:, e * P:e * P + P], ones[:, :], gateT[:, e:e + 1], sign, ALU.mult, ALU.mult)
            dve.drain()
            dve.tensor_copy(gate_hi[:, :], ctx_n[:, 0:2 * P])
            dve.drain()
            dve.tensor_tensor(gate_lo[:, :], ctx_n[:, 0:2 * P], gate_hi[:, :], ALU.subtract)
            dve.tensor_tensor(b2T[:, 3:4], b2T[:, 0:1], b2T[:, 1:2], ALU.add)
            dve.drain()
            dve.tensor_tensor(b2T[:, 4:5], b2T[:, 3:4], b2T[:, 2:3], ALU.add)
            dve.drain()
            dve.tensor_scalar(b2g[:, :], gates[:, 4 * B:5 * B], b2T[:, 4:5], None, ALU.mult).then_inc(setup_dve, 1)
            for k, (o, n, _) in enumerate(w_pieces[ATTN_PIECES:]):
                dve.wait_ge(w_hi_done, ATTN_PIECES + k + 1)
                dve.tensor_tensor(w_part(w_lo, o, n), w_source(o, n), w_part(w_hi, o, n),
                                  ALU.subtract).then_inc(w_lo_done, 1)

            def top(n, hh, t):
                if t == 0 and not (isinstance(n, int) and n == 0):
                    dve.wait_ge(topT_done, 2 * n - 1 + hh)
                dve.wait_ge(tops_done, 8 * n + 4 * hh + t + 1)
                dve.reduce_max(row_max[:, hh * TPB + t:hh * TPB + t + 1], s_bank(t)[:, :], AXX).then_inc(top_done, 1)

            def lo(n, hh, kt):
                if kt in POOL_LO:
                    return
                o = (hh * TPB + kt) * S
                dve.wait_ge(band_done, 8 * n + 4 * hh + kt + 1)
                dve.tensor_tensor(probs_lo[:, o:o + S], probs[:, o:o + S],
                                  probs[:, o:o + S].bitcast(BF16)[:, 1:2 * S:2], ALU.subtract).then_inc(lo_dve, 1)

            def pair_lo_part(n, k):
                dve.wait_ge(qkv_hi, 3 * n + k + 1)
                dve.tensor_tensor(pair_lo[:, k * S:k * S + S], PROJ[:, :], pair_hi[:, k * S:k * S + S],
                                  ALU.subtract).then_inc(qkv_lo, 1)

            def v_lo_part(n, ring):
                dve.wait_ge(qkv_hi, 3 * n + 3)
                o, ol = ring * 2 * TPB * VP, ring * 2 * TPB * DK
                dve.tensor_tensor(v_lo[:, ol:ol + 2 * TPB * DK].rearrange("p (a c) -> p a c", c=DK),
                                  PROJ[:, :].rearrange("p (a c) -> p a c", c=DK),
                                  v_hi[:, o:o + 2 * TPB * VP].rearrange("p (a c) -> p a c", c=VP)[:, :, 0:DK],
                                  ALU.subtract).then_inc(qkv_lo, 1)

            def normalise(n, hh):
                pvv = PV[:, 0:TPB * (DK + 1)].rearrange("p (t c) -> p t c", c=DK + 1)
                dve.wait_ge(pv_done, 2 * n + hh + 1)
                dve.reciprocal(recip[:, :].unsqueeze(2), pvv[:, :, DK:DK + 1]).then_inc(recip_done, 1)
                dve.wait_ge(recip_done, 2 * n + hh + 1)
                if hh == 0 and not is_at(n, 0):
                    dve.wait_ge(ctxT_done, n)
                dve.tensor_tensor(ctx_n[:, :].rearrange("p (t c) -> p t c", c=P)[:, :, hh * DK:hh * DK + DK],
                                  pvv[:, :, 0:DK], recip[:, :].unsqueeze(2).to_broadcast([P, TPB, DK]),
                                  ALU.mult).then_inc(norm_done, 1)

            def iteration(it, i):
                project, rate = not is_at(it, ITERS - 2) and not is_at(it, ITERS - 1), not is_at(it, ITERS - 1)
                top(it, 1, 0)
                top(it, 1, 1)
                if rate:
                    v_lo_part(it + 1, (i + 1) % RING)
                top(it, 1, 2)
                top(it, 1, 3)
                if not rate:
                    add_attention(0)
                    dve.wait_ge(resid, 1)
                    row_stats(0, 0)
                    dve.wait_ge(ln[1]["stats"], TPB)
                    variances(0, 0)
                if not is_at(it, 0):
                    normalise(it - 1, 0)
                if project:
                    pair_lo_part(it + 2, 0)
                for kt in DVE_LO:
                    lo(it, 0, kt)
                if not rate:
                    normalise_rows(0, 0)
                if rate:
                    top(it + 1, 0, 0)
                    top(it + 1, 0, 1)
                if project:
                    pair_lo_part(it + 2, 1)
                if rate:
                    top(it + 1, 0, 2)
                    top(it + 1, 0, 3)
                if not is_at(it, 0):
                    normalise(it - 1, 1)
                for kt in DVE_LO:
                    lo(it, 1, kt)

            pair_lo_part(0, 0)
            pair_lo_part(0, 1)
            v_lo_part(0, 0)
            for t in range(TPB):
                top(0, 0, t)
            pair_lo_part(1, 0)
            pair_lo_part(1, 1)
            attention(dve, iteration)
            normalise(ITERS - 1, 0)
            normalise(ITERS - 1, 1)

            def mask(b, e):
                dve.wait_ge(gate_done, b + 1)
                for k, src in enumerate((hT_hi, hT_lo)):
                    o = (2 * e + k) * S
                    dve.scalar_tensor_tensor(xm[:, o:o + S], bank[3][:, :], 0.0, src[:, bass.ds(b * S, S)],
                                             ALU.is_gt if e == 1 else ALU.is_le, ALU.mult).then_inc(masked, 1)

            def block_output(b):
                dve.wait_ge(moe_back, b + 1)
                xb = x[:, bass.ds(b * S, S)]
                dve.tensor_tensor(xb, xb, bank[4][:, :], ALU.add).then_inc(y_done, 1)

            def experts(b, par):
                more = not is_at(b, B - 1)
                for c in range(CHUNKS):
                    o = (c % 4) * S
                    if c == 5 and more:
                        dve.wait_ge(resid, b + 2)
                    if c == 6 and more:
                        dve.wait_ge(ln[1]["stats"], (b + 2) * TPB)
                    dve.wait_ge(hid_done, CHUNKS * b + c + 1)
                    dve.tensor_tensor(hid_lo[:, o:o + S], hid[:, o:o + S],
                                      hid[:, o:o + S].bitcast(BF16)[:, 1:2 * S:2],
                                      ALU.subtract).then_inc(hid_lo_done, 1)
                    if c < 2:
                        mask(b, c)
                    if c == 3 and not is_at(b, 0):
                        block_output(b - 1)
                    if c == 4 and more:
                        add_attention(b + 1)
                    if c == 5 and more:
                        row_stats(b + 1, 1 - par)
                    if c == 6 and more:
                        variances(b + 1, 1 - par)
                    if c == 7 and more:
                        normalise_rows(b + 1, 1 - par)

            batches(dve, experts)
            block_output(B - 1)

        @block.tensor
        def _(pe):
            pe.wait_ge(wmod_in, 16)
            pe.wait_ge(setup_dve, 6)
            for i in range(6):
                mm = pe.matmul(PROJ[:, i * B:i * B + B], wmod[:, i * D:i * D + D], cT[:, B:2 * B],
                               start=True, stop=True)
            mm.then_inc(setup_pe, 1)
            pe.wait_ge(consts_in, 16 * 4)
            pe.matmul(TURN[0:H, 0:OFFS], rel[:, :], onehot[:, :], start=True, stop=True).then_inc(setup_pe, 1)
            pe.matmul(WOUT[:, 0:H], select[:, :], rel[:, :], start=True, stop=True).then_inc(setup_pe, 1)

            def layernorm():
                s = ln[0]
                with pe.Fori(0, B // 2) as j:
                    for par in range(2):
                        b = 2 * j + par
                        pe.wait_ge(s["h32"], 2 * j)
                        pe.wait_ge(s["xn"], TPB * b + TPB)
                        for t in range(TPB):
                            o = par * S + t * P
                            mm = pe.transpose(bank[par][:, t * P:t * P + P], xn[0][:, o:o + P], ident[:, :])
                        mm.then_inc(s["xT"], 1)

            def turn_back(b, src):
                for t in range(TPB):
                    mm = pe.transpose(PROJ[:, t * P:t * P + P], src[:, t * P:t * P + P], ident[:, :])
                mm.then_inc(attn_back, 1)

            def turn_rows(b):
                pe.wait_ge(resid, b + 1)
                pe.wait_ge(ln[1]["xn"], TPB * b + TPB)
                for t in range(TPB):
                    mm = pe.transpose(PROJ[:, t * P:t * P + P], xn[1][:, t * P:t * P + P], ident[:, :])
                mm.then_inc(ln[1]["xT"], 1)

            layernorm()

            def q_or_k(n, w, count):
                b, g = (n >> 3) & (B - 1), n & (PAIRS - 1)
                if not (isinstance(n, int) and n == 0 and count == 0):
                    pe.wait_ge(qkv_lo, 3 * n + count)
                h_hi, h_lo = hT_hi[:, bass.ds(b * S, S)], hT_lo[:, bass.ds(b * S, S)]
                pe.matmul(PROJ[:, :], w_hi[:, bass.ds(w + g * P, P)], h_hi, start=True, stop=False)
                pe.matmul(PROJ[:, :], w_lo[:, bass.ds(w + g * P, P)], h_hi, start=False, stop=False)
                pe.matmul(PROJ[:, :], w_hi[:, bass.ds(w + g * P, P)], h_lo, start=False,
                          stop=True).then_inc(proj_done, 1)

            def v_proj(n):
                b, g = (n >> 3) & (B - 1), n & (PAIRS - 1)
                pe.wait_ge(qkv_lo, 3 * n + 2)
                wv_hi, wv_lo = w_hi[:, bass.ds(WV + g * P, P)], w_lo[:, bass.ds(WV + g * P, P)]
                for t in range(TPB):
                    o = PROJ[:, t * P:t * P + P]
                    h_hi, h_lo = hT_hi[:, bass.ds(b * S + t * P, P)], hT_lo[:, bass.ds(b * S + t * P, P)]
                    pe.matmul(o, h_hi, wv_hi, start=True, stop=False)
                    pe.matmul(o, h_hi, wv_lo, start=False, stop=False)
                    mm = pe.matmul(o, h_lo, wv_hi, start=False, stop=True)
                mm.then_inc(proj_done, 1)

            def rough_scores(n, ring, hh, t):
                idx = 8 * n + 4 * hh + t
                o = slot(ring, hh)
                if not (isinstance(n, int) and n == 0) or hh or t >= 2:
                    pe.wait_ge(top_done, idx - 1)
                if hh == 0 and t == 0:
                    pe.wait_ge(spread_a, 64 * n + 64)
                pe.matmul(s_bank(t)[:, :], q_hilo[:, o + t * P:o + t * P + P], k_hihi[:, o:o + S],
                          start=True, stop=True).then_inc(tops_done, 1)

            def scores(n, ring, hh, kt):
                idx = 8 * n + 4 * hh + kt
                o = slot(ring, hh)
                if not (isinstance(n, int) and n == 0) or hh or kt >= 2:
                    pe.wait_ge(exp_done, idx - 1)
                pe.matmul(st_bank(kt)[:, :], k_hihi[:, o + kt * P:o + kt * P + P], q_hilo[:, o:o + S],
                          start=True, stop=False)
                if kt == 0:
                    pe.wait_ge(mrow_in[hh], 16 * n + 16)
                    if hh == 0:
                        pe.wait_ge(spread_b, 32 * n + 32)
                pe.matmul(st_bank(kt)[:, :],
                          k_lo[:, bass.ds(((n & (PAIRS - 1)) * 2 + hh) * S + kt * P, P)],
                          q_ext[:, o:o + S], start=False, stop=True).then_inc(scores_done, 1)

            def turn_tops(n, hh):
                pe.wait_ge(top_done, 8 * n + 4 * hh + 4)
                if hh == 0:
                    if not is_at(n, 0):
                        pe.wait_ge(mrow_done, 2 * n)
                elif not isinstance(n, int) or n > 1:
                    pe.wait_ge(ctx_out, n - 1)
                else:
                    pe.wait_ge(mrow_done, 2 * n + 1)
                pe.transpose(TURN[0:TPB, 0:P], row_max[:, hh * TPB:hh * TPB + TPB], ident[:, :]).then_inc(topT_done, 1)

            def attend(n, ring, hh):
                pe.wait_ge(lo_dve, (2 * n + hh + 1) * len(DVE_LO))
                pe.wait_ge(lo_pool, (2 * n + hh + 1) * len(POOL_LO))
                pe.wait_ge(qkv_lo, 3 * n + 3)
                if not (is_at(n, 0) and hh == 0):
                    pe.wait_ge(norm_done, 2 * n + hh)
                for t in range(TPB):
                    o = t * (DK + 1)
                    for kt in range(TPB):
                        a = (ring * TPB + kt) * 2 + hh
                        vh, vl = v_hi[:, a * VP:a * VP + DK + 1], v_lo[:, a * DK:a * DK + DK]
                        pcol = (hh * TPB + kt) * S + t * P
                        p_hi = probs[:, pcol:pcol + P].bitcast(BF16)[:, 1:2 * P:2]
                        pe.matmul(PV[:, o:o + DK + 1], p_hi, vh, start=kt == 0, stop=False)
                        pe.matmul(PV[:, o:o + DK], p_hi, vl, start=False, stop=False)
                        mm = pe.matmul(PV[:, o:o + DK + 1], probs_lo[:, pcol:pcol + P], vh, start=False,
                                       stop=kt == TPB - 1)
                mm.then_inc(pv_done, 1)

            def turn_context(n):
                pe.wait_ge(norm_done, 2 * n + 2)
                if is_at(n, ITERS - 1):
                    pe.wait_ge(ctx_out, ITERS - 1)
                elif is_at(n, ITERS - 2):
                    pe.wait_ge(mrow_done, 2 * ITERS)
                else:
                    pe.wait_ge(mrow_done, 2 * n + 5)
                for t in range(TPB):
                    mm = pe.transpose(TURN[:, t * P:t * P + P], ctx_n[:, t * P:t * P + P], ident[:, :])
                mm.then_inc(ctxT_done, 1)

            def out_product(n, odd):
                g = n & (PAIRS - 1)
                c_hi = ctxT[:, :].bitcast(BF16)[:, 1:2 * S:2]
                pe.wait_ge(ctx_lo, n + 1)
                if not odd:
                    pe.wait_ge(wout_read, (n >> 1) + 1)
                pe.matmul(WOUT[:, :], w_hi[:, bass.ds(WO + g * P, P)], c_hi, start=not odd, stop=False)
                pe.matmul(WOUT[:, :], w_lo[:, bass.ds(WO + g * P, P)], c_hi, start=False, stop=False)
                pe.matmul(WOUT[:, :], w_hi[:, bass.ds(WO + g * P, P)], ctxT_lo[:, :], start=False,
                          stop=odd).then_inc(wo_done, 1)

            def iteration(it, i):
                ring, nxt, nring = i % RING, it + 1, (i + 1) % RING
                after, last = not is_at(it, 0), is_at(it, ITERS - 1)
                project, rate = not last and not is_at(it, ITERS - 2), not last
                scores(it, ring, 0, 0)
                scores(it, ring, 0, 1)
                rough_scores(it, ring, 1, 2)
                rough_scores(it, ring, 1, 3)
                if project:
                    q_or_k(it + 2, WQ, 0)
                if last:
                    pe.wait_ge(summed, 1 + PAIRS // 2)
                    turn_back(0, attn_T[:, 0:S])
                scores(it, ring, 0, 2)
                scores(it, ring, 0, 3)
                turn_tops(it, 1)
                if rate:
                    rough_scores(nxt, nring, 0, 0)
                    rough_scores(nxt, nring, 0, 1)
                if after:
                    attend(it - 1, (i - 1) % RING, 1)
                if project:
                    q_or_k(it + 2, WK, 1)
                if after and not is_at(it, 1):
                    out_product(it - 2, odd=i % 2 == 1)
                scores(it, ring, 1, 0)
                scores(it, ring, 1, 1)
                if rate:
                    rough_scores(nxt, nring, 0, 2)
                    rough_scores(nxt, nring, 0, 3)
                scores(it, ring, 1, 2)
                scores(it, ring, 1, 3)
                if rate:
                    turn_tops(nxt, 0)
                    rough_scores(nxt, nring, 1, 0)
                    rough_scores(nxt, nring, 1, 1)
                if last:
                    turn_rows(0)
                attend(it, ring, 0)
                if project:
                    v_proj(it + 2)
                if after:
                    turn_context(it - 1)

            pe.wait_ge(ln[0]["lo"], B)
            pe.wait_ge(w_lo_done, ATTN_PIECES)
            pe.wait_ge(setup_dve, 8)
            q_or_k(0, WQ, 0)
            q_or_k(0, WK, 1)
            v_proj(0)
            for t in range(TPB):
                rough_scores(0, 0, 0, t)
            pe.wait_ge(setup_act, 3)
            turn_tops(0, 0)
            q_or_k(1, WQ, 0)
            q_or_k(1, WK, 1)
            v_proj(1)
            rough_scores(0, 0, 1, 0)
            rough_scores(0, 0, 1, 1)
            pe.wait_ge(far_in, 16 * 2 * RING)
            pe.wait_ge(far_rows, 1)
            attention(pe, iteration)

            def up(b, c):
                e = (2, 0, 1)[c // HC]
                w = W1 + e * HID + (c % HC) * P
                if e == 2:
                    x_hi, x_lo = hT_hi[:, bass.ds(b * S, S)], hT_lo[:, bass.ds(b * S, S)]
                else:
                    x_hi, x_lo = xm[:, 2 * e * S:2 * e * S + S], xm[:, (2 * e + 1) * S:(2 * e + 2) * S]
                    if c % HC == 0:
                        pe.wait_ge(masked, 4 * b + 2 * e + 2)
                hb = bank[c % 2]
                if c >= 2:
                    pe.wait_ge(hid_done, CHUNKS * b + c - 1)
                elif is_at(b, 0):
                    pe.wait_ge(exp_done, 8 * ITERS)
                else:
                    pe.wait_ge(hid_done, CHUNKS * b)
                pe.matmul(hb[:, :], w_hi[:, w:w + P], x_hi, start=True, stop=False)
                pe.matmul(hb[:, :], w_lo[:, w:w + P], x_hi, start=False, stop=False)
                pe.matmul(hb[:, :], w_hi[:, w:w + P], x_lo, start=False, stop=True).then_inc(up_done, 1)

            def down(b, c):
                e = (2, 0, 1)[c // HC]
                w = W2 + (e * HC + c % HC) * D
                o = (c % 4) * S
                h_hi = hid[:, o:o + S].bitcast(BF16)[:, 1:2 * S:2]
                pe.wait_ge(hid_lo_done, CHUNKS * b + c + 1)
                if c == 0 and not is_at(b, 0):
                    pe.wait_ge(moe_done, b)
                pe.matmul(bank[2][:, :], w_hi[:, w:w + P], h_hi, start=c == 0, stop=False)
                pe.matmul(bank[2][:, :], w_lo[:, w:w + P], h_hi, start=False, stop=False)
                pe.matmul(bank[2][:, :], w_hi[:, w:w + P], hid_lo[:, o:o + S], start=False,
                          stop=c == CHUNKS - 1).then_inc(down_done, 1)

            def gate(b):
                pe.wait_ge(ln[1]["lo"], b + 1)
                if not is_at(b, 0):
                    pe.wait_ge(masked, 4 * b)
                for e in range(2):
                    g_hi, g_lo = gate_hi[:, e * P:e * P + P], gate_lo[:, e * P:e * P + P]
                    h_hi, h_lo = hT_hi[:, bass.ds(b * S, S)], hT_lo[:, bass.ds(b * S, S)]
                    pe.matmul(bank[3][:, :], g_hi, h_hi, start=e == 0, stop=False)
                    pe.matmul(bank[3][:, :], g_lo, h_hi, start=False, stop=False)
                    mm = pe.matmul(bank[3][:, :], g_hi, h_lo, start=False, stop=e == 1)
                mm.then_inc(gate_done, 1)

            def turn_moe(b):
                pe.wait_ge(moe_done, b + 1)
                if is_at(b, 0):
                    pe.wait_ge(norm_done, 2 * ITERS)
                else:
                    pe.wait_ge(y_done, b)
                for t in range(TPB):
                    mm = pe.transpose(bank[4][:, t * P:t * P + P], moe_T[:, t * P:t * P + P], ident[:, :])
                mm.then_inc(moe_back, 1)

            def experts(b, par):
                more = not is_at(b, B - 1)
                gate(b)
                if is_at(b, 0):
                    attend(ITERS - 1, (ITERS - 1) % RING, 1)
                    out_product(ITERS - 2, odd=False)
                for c in range(CHUNKS + 2):
                    if c < CHUNKS:
                        up(b, c)
                    if c == 0 and is_at(b, 0):
                        turn_context(ITERS - 1)
                    if c == 2 and is_at(b, 0):
                        out_product(ITERS - 1, odd=True)
                    if c >= 2:
                        down(b, c - 2)
                    if c == 2 and not is_at(b, 0):
                        turn_moe(b - 1)
                    if c == 4 and more:
                        pe.wait_ge(back_in, b + 1)
                        pe.wait_ge(ln[1]["h32"], b + 1)
                        turn_back(b + 1, back_T)
                    if c == 9 and more:
                        turn_rows(b + 1)

            pe.wait_ge(w_lo_done, len(w_pieces))
            pe.wait_ge(setup_dve, 13)
            pe.wait_ge(top_done, 8 * ITERS)
            batches(pe, experts)
            turn_moe(B - 1)


_INS = ['L0_attn_x', 'L0_attn_Wq', 'L0_attn_Wk', 'L0_attn_Wv', 'L0_attn_Wo', 'L0_attn_rel_emb', 'L0_ffn_gate_w',
        'L0_ffn_w1', 'L0_ffn_b1', 'L0_ffn_w2', 'L0_ffn_b2', 'L0_ffn_sw1', 'L0_ffn_sb1', 'L0_ffn_sw2', 'L0_ffn_sb2',
        'L0_c', 'L0_wmod']


def kernel(**inputs):
    import concourse.bacc as bacc
    from concourse.bass_utils import run_bass_kernel_spmd

    nc = bacc.Bacc("TRN2", target_bir_lowering=False, num_devices=1)
    arrays, ins, consts = {}, {}, {}
    for name in _INS:
        a = np.ascontiguousarray(inputs[name])
        arrays[f"in_{name}"] = a
        ins[name] = nc.dram_tensor(f"in_{name}", a.shape, mybir.dt.from_np(a.dtype), kind="ExternalInput").ap()
    for name, a in shape_constants().items():
        arrays[f"const_{name}"] = a
        consts[name] = nc.dram_tensor(f"const_{name}", a.shape, mybir.dt.from_np(a.dtype), kind="ExternalInput").ap()
    out = nc.dram_tensor("out_y", (B, S, D), F32, kind="ExternalOutput").ap()
    adaln_program(nc, ins, consts, out)
    r = run_bass_kernel_spmd(nc, [arrays], core_ids=[0])
    return r.results[0]["out_y"]
```

```python
from contextlib import ExitStack

import numpy as np

import concourse.bass as bass
from concourse import mybir

F32 = mybir.dt.float32
F16 = mybir.dt.float16
BF16 = mybir.dt.bfloat16
ALU = mybir.AluOpType
ACT = mybir.ActivationFunctionType
AXX = mybir.AxisListType.X

P = 128
B, S, D = 8, 512, 128
H, DK = 16, 64
TPB = S // P
TILES = B * TPB
PAIRS = H // 2
ITERS = B * PAIRS
RING = 3
UNROLL = 6
LOOPS = (ITERS - 4) // UNROLL
HID, EXPERTS = 512, 3
HC = HID // P
CHUNKS = EXPERTS * HC
EPS = 1e-5
BUCKETS, EXACT = 32, 8
FAR = 91
BAND = 2 * FAR + P - 2
OFFS = 2 * (FAR + P - 2) + 1
M_ROW = DK
M_SCALE = 32.0
FAR_ROW = M_ROW + 1

WQ, WK, WV, WO = 0, 1024, 2048, 3072
W1 = 4096
W2 = W1 + EXPERTS * HID
WCOLS = W2 + EXPERTS * HC * D

POOL_LO = ((3,), (2, 3))
DVE_LO = ((0, 1, 2), (0, 1))


def lo_count(tiles, n, hh):
    both = len(tiles[0]) + len(tiles[1])
    return both * n + (len(tiles[0]) if hh == 0 else both)


def band_of(kt):
    first = P * kt - FAR + 1
    q0, q1 = max(0, first), min(S, first + BAND)
    return q0, q1, q0 - first


def bucket_of(n):
    a = abs(n)
    b = a if a < EXACT else EXACT + sum(a * a >= 64 * 2 ** j for j in range(1, EXACT))
    return b + (BUCKETS // 2 if n < 0 else 0)


def shape_constants():
    onehot = np.zeros((BUCKETS, OFFS), np.float32)
    for m in range(OFFS):
        onehot[bucket_of(m - OFFS // 2), m] = 1
    select = np.zeros((BUCKETS, P), np.float32)
    rowmask = np.zeros((P, 3 + TPB), np.float32)
    indicator = np.zeros((P, S), np.float16)
    rowmask[M_ROW, 2] = M_SCALE
    rowmask[M_ROW, 3:] = 1
    q = np.arange(S)
    for j in range(TPB):
        for side in range(2):
            for part in range(2):
                r = FAR_ROW + 4 * j + 2 * side + part
                select[bucket_of(-FAR if side == 0 else FAR), r] = 1
                rowmask[r, part] = 1
                rowmask[r, 3 + j] = 1
                indicator[r] = (q <= P * j - FAR) if side == 0 else (q >= P * j + P - 1 + FAR)
    return {"tables": np.concatenate([np.eye(P, dtype=np.float32), rowmask], axis=1),
            "buckets": np.concatenate([onehot, select], axis=1), "indicator": indicator}


def adaln_program(nc, ins, consts, out):
    x_d = ins["L0_attn_x"].rearrange("b s d -> (b s) d").rearrange("(t p) d -> p t d", p=P)
    out_d = out.rearrange("b s d -> (b s) d").rearrange("(t p) d -> p t d", p=P)
    bias_scratch = nc.dram_tensor("bias_scratch", (P, H, OFFS), F32, kind="Internal").ap()

    ctx = ExitStack()
    with ctx:
        ctx.enter_context(nc.allow_non_contiguous_dma(reason="small transposed vectors"))

        def sb(name, shape, dt=F32):
            return ctx.enter_context(nc.sbuf_tensor(name, shape, dt))

        def sem(name):
            return ctx.enter_context(nc.semaphore(name))

        bank = [ctx.enter_context(nc.psum_tensor(f"bank{i}", [P, 512], F32)) for i in range(8)]

        x = sb("x", [P, TILES * D])
        hT_hi = sb("hT_hi", [P, B * S], F16)
        hT_lo = sb("hT_lo", [P, B * S], F16)
        w_raw = sb("w_raw", [P, WCOLS])
        w_hi = sb("w_hi", [P, WCOLS], F16)
        w_lo = sb("w_lo", [P, WCOLS], F16)
        attn_T = w_raw[:, 0:B * S]
        k_lo = sb("k_lo", [P, H * S], F16)
        exp_bias = sb("exp_bias", [P, H * BAND])
        pair_hi = sb("pair_hi", [P, 2 * S], F16)
        pair_lo = sb("pair_lo", [P, 2 * S], F16)
        q_hilo = sb("q_hilo", [P, RING * 2 * S], F16)
        q_ext = sb("q_ext", [P, RING * 2 * S], F16)
        k_hihi = sb("k_hihi", [P, RING * 2 * S], F16)
        VP = DK + 2
        v_hi = sb("v_hi", [P, RING * 2 * TPB * VP], F16)
        v_lo = sb("v_lo", [P, RING * 2 * TPB * DK], F16)
        probs = sb("probs", [P, 2 * TPB * S])
        probs_lo = sb("probs_lo", [P, 2 * TPB * S], F16)
        row_max = sb("row_max", [P, 2 * TPB])
        max_row = sb("max_row", [TPB, 2 * P], F16)
        recip = sb("recip", [P, TPB])
        ctx_n = sb("ctx_n", [P, TPB * P])
        ctxT = sb("ctxT", [P, S])
        ctxT_lo = sb("ctxT_lo", [P, S], F16)
        attn_part = sb("attn_part", [P, S])
        tables = sb("tables", [P, P + 3 + TPB])
        ident, rowmask = tables[:, 0:P], tables[:, P:P + 3 + TPB]
        buckets = sb("buckets", [BUCKETS, OFFS + P])
        onehot, select = buckets[:, 0:OFFS], buckets[:, OFFS:OFFS + P]
        relT = sb("relT", [H, BUCKETS])
        rel_top = sb("rel_top", [H, 1])
        rel = sb("rel", [BUCKETS, H])
        eb_row = sb("eb_row", [H, OFFS])
        far = sb("far", [P, 3 * H])
        far_hi = sb("far_hi", [P, H], F16)
        far_tile = sb("far_tile", [P, H * TPB])
        cT = sb("cT", [P, 3 * B])
        wmod = sb("wmod", [P, 6 * D])
        mod = sb("mod", [P, 6 * B])
        gates = sb("gates", [P, 2 * 4 * B])
        b1T = sb("b1T", [P, CHUNKS])
        b2T = sb("b2T", [P, EXPERTS + 2])
        b2g = sb("b2g", [P, B])
        gateT = sb("gateT", [P, 2])
        ones = sb("ones", [P, P])
        gate_hi = sb("gate_hi", [P, 2 * P], F16)
        gate_lo = sb("gate_lo", [P, 2 * P], F16)
        stats = sb("stats", [P, TILES * 6])
        mean_var = sb("mean_var", [P, TILES * 2])
        var_eps = sb("var_eps", [P, TILES])
        minus_half = sb("minus_half", [P, TILES])
        rstd = sb("rstd", [P, TILES])
        xn = [w_raw[:, W1:W1 + 2 * S], pair_hi[:, :].bitcast(F32)]
        h32 = [w_raw[:, W1 + 2 * S:W1 + 4 * S], pair_lo[:, :].bitcast(F32)]
        hid = probs[:, 0:4 * S]
        hid_lo = probs_lo[:, 0:4 * S]
        xm = probs_lo[:, 4 * S:8 * S]
        moe_T = ctx_n
        back_T = ctxT

        def mod_col(i, b):
            return mod[:, bass.ds(i * B + b, 1)]

        (tables_in, buckets_in, x0_in, x_in, c_in, rel_in, ffn_small_in, wq_in, wk_in, wv_in, wo_in, ffn_w_in, wmod_in,
         bias_out, bias_in, far_in, spread_a, spread_b, stored) = map(
            sem, ("tables_in", "buckets_in", "x0_in", "x_in", "c_in", "rel_in", "ffn_small_in", "wq_in", "wk_in",
                  "wv_in", "wo_in", "ffn_w_in", "wmod_in", "bias_out", "bias_in", "far_in", "spread_a", "spread_b",
                  "stored"))
        mrow_in = [sem("mrow_in0"), sem("mrow_in1")]
        silu = sem("silu")
        mod_mm, mod_out, mod_ready = sem("mod_mm"), sem("mod_out"), sem("mod_ready")
        rel_step, rel_turned, rel_mm, bias_row = sem("rel_step"), sem("rel_turned"), sem("rel_mm"), sem("bias_row")
        far_step, far_rows, gates_ready = sem("far_step"), sem("far_rows"), sem("gates_ready")
        ffn_ready = sem("ffn_ready")
        w_hi_done, w_lo_done = sem("w_hi_done"), sem("w_lo_done")
        ones_in_v, halves, ones_filled = sem("ones_in_v"), sem("halves"), sem("ones_filled")
        ln = [{k: sem(f"ln{ph}_{k}") for k in ("stats", "aggr", "eps", "rstd", "xn", "xT", "h32", "hi", "lo")}
              for ph in range(2)]
        (proj_done, scores_done, tops_done, top_done, topT_done, mrow_done, qkv_hi, qkv_lo, exp_done, band_done,
         lo_dve, lo_pool, pv_done, recip_done, norm_done, ctxT_done, ctx_out, ctx_lo, wo_done, wout_read,
         summed) = map(sem, ("proj_done", "scores_done", "tops_done", "top_done", "topT_done", "mrow_done", "qkv_hi",
                             "qkv_lo", "exp_done", "band_done", "lo_dve", "lo_pool", "pv_done", "recip_done",
                             "norm_done", "ctxT_done", "ctx_out", "ctx_lo", "wo_done", "wout_read", "summed"))
        back_in, attn_back, resid = sem("back_in"), sem("attn_back"), sem("resid")
        (gate_done, masked, up_done, hid_done, hid_lo_done, down_done, moe_done, moe_back, y_done) = map(
            sem, ("gate_done", "masked", "up_done", "hid_done", "hid_lo_done", "down_done", "moe_done", "moe_back",
                  "y_done"))

        block = ctx.enter_context(nc.Block())

        def st_bank(kt):
            return bank[kt % 2]

        def s_bank(t):
            return bank[2 + t % 2]

        PV, PROJ, TURN, WOUT = bank[4], bank[5], bank[6], bank[7]

        def slot(ring, hh):
            return (2 * ring + hh) * S

        def attention(eng, iteration):
            iteration(0, 0)
            iteration(1, 1)
            with eng.Fori(0, LOOPS) as j:
                for u in range(UNROLL):
                    iteration(UNROLL * j + 2 + u, 2 + u)
            iteration(ITERS - 2, ITERS - 2)
            iteration(ITERS - 1, ITERS - 1)

        def batches(eng, experts):
            experts(0, 0)
            with eng.Fori(0, B // 2 - 1) as j:
                for u in range(2):
                    experts(2 * j + 1 + u, (1 + u) % 2)
            experts(B - 1, 1)

        FIRST_LN = 4

        def ln_bank(b):
            return bank[b % 2] if b < FIRST_LN else WOUT

        def is_at(it, n):
            return isinstance(it, int) and it == n

        FIRST = 2 * P
        w_pieces = [(WQ, FIRST), (WK, FIRST), (WV, FIRST), (WQ + FIRST, 1024 - FIRST), (WK + FIRST, 1024 - FIRST),
                    (WV + FIRST, 1024 - FIRST), (WO, 1024), (W1, 1024), (W1 + 1024, 512), (W2, 1024), (W2 + 1024, 512)]
        w_piece_in = [(wq_in, 16), (wk_in, 16), (wv_in, 16), (wq_in, 16), (wk_in, 16), (wv_in, 16), (wo_in, 16)] + [
            (ffn_w_in, 64)] * 4
        ATTN_PIECES = 7

        def w_part(t, o, n):
            if o < WV:
                return t[:, o:o + n].rearrange("p (g d h) -> p g h d", h=2, d=DK)
            return t[:, o:o + n]

        def w_source(o, n):
            if o < WV:
                return w_raw[:, o:o + n].rearrange("p (g h d) -> p g h d", h=2, d=DK)
            return w_raw[:, o:o + n]

        def w_view(o, src):
            n = src.shape[-1] if len(src.shape) == 2 else src.shape[-1] * src.shape[-2]
            t = w_raw[:, o:o + n]
            return t if len(src.shape) == 2 else t.rearrange("p (g n) -> p g n", n=src.shape[-1])

        @block.sync
        def _(sp):
            def load(o, src, done):
                sp.dma_start(w_view(o, src), src).then_inc(done, 16)

            sp.dma_start(x[:, 0:S].rearrange("p (t d) -> p t d", d=D), x_d[:, 0:TPB, :]).then_inc(x0_in, 16)
            load(WQ, ins["L0_attn_Wq"], wq_in)
            load(WK, ins["L0_attn_Wk"], wk_in)
            sp.dma_start(wmod[:, :], ins["L0_wmod"]).then_inc(wmod_in, 16)
            load(WV, ins["L0_attn_Wv"], wv_in)

            BH = H // 4

            def biases_out(k):
                sp.dma_start(bias_scratch.rearrange("p h m -> h p m")[k * BH:k * BH + BH],
                             eb_row[k * BH:k * BH + BH, :].unsqueeze(1).to_broadcast([BH, P, OFFS])
                             ).then_inc(bias_out, 16)

            def biases_in(k, pieces_out):
                sp.wait_ge(bias_out, 16 * pieces_out)
                toeplitz = bass.AP(tensor=bias_scratch.tensor,
                                   offset=bias_scratch.offset + k * BH * OFFS + P - 1,
                                   ap=[[H * OFFS - 1, P], [OFFS, BH], [1, BAND]])
                sp.dma_start(exp_bias[:, k * BH * BAND:(k + 1) * BH * BAND].rearrange("p (h c) -> p h c", h=BH),
                             toeplitz).then_inc(bias_in, 16)

            sp.wait_ge(bias_row, 1)
            biases_out(0)
            sp.dma_start(x[:, S:B * S].rearrange("p (t d) -> p t d", d=D), x_d[:, TPB:TILES, :]).then_inc(x_in, 16)
            biases_in(0, 1)
            load(WO, ins["L0_attn_Wo"].rearrange("(g p) n -> p g n", p=P), wo_in)

            def max_row_in(n, ring, hh):
                sp.wait_ge(mrow_done, 2 * n + hh + 1)
                o = slot(ring, hh)
                sp.dma_start(q_ext[M_ROW:M_ROW + 1, o:o + S].rearrange("o (t c) -> o t c", c=P),
                             max_row[:, hh * P:hh * P + P]).then_inc(mrow_in[hh], 16)

            def spread(dst, src, done):
                sp.dma_start(dst.rearrange("p (h c) -> p h c", h=2), src).then_inc(done, 16)

            def spread_q(n, ring):
                o = slot(ring, 0)
                sp.wait_ge(qkv_hi, 3 * n + 1)
                spread(q_hilo[0:DK, o:o + 2 * S], pair_hi[:, 0:S], spread_a)
                spread(q_ext[0:DK, o:o + 2 * S], pair_hi[:, 0:S], spread_b)
                sp.wait_ge(qkv_lo, 3 * n + 1)
                spread(q_hilo[DK:P, o:o + 2 * S], pair_lo[:, 0:S], spread_a)

            def spread_k(n, ring):
                o = slot(ring, 0)
                sp.wait_ge(qkv_hi, 3 * n + 2)
                spread(k_hihi[0:DK, o:o + 2 * S], pair_hi[:, S:2 * S], spread_a)
                spread(k_hihi[DK:P, o:o + 2 * S], pair_hi[:, S:2 * S], spread_a)
                sp.wait_ge(qkv_lo, 3 * n + 2)
                at = (((n + PAIRS) << 1) & (2 * PAIRS - 2)) << 9
                spread(k_lo[0:DK, bass.ds(at, 2 * S)], pair_lo[:, S:2 * S], spread_b)

            def iteration(it, i):
                max_row_in(it, i % RING, 1)
                if not is_at(it, ITERS - 2) and not is_at(it, ITERS - 1):
                    spread_q(it + 2, (i + 2) % RING)
                    spread_k(it + 2, (i + 2) % RING)
                if not is_at(it, ITERS - 1):
                    max_row_in(it + 1, (i + 1) % RING, 0)
                if is_at(it, 0):
                    for k in range(1, 4):
                        biases_in(k, 4)
                if is_at(it, 1):
                    sp.wait_ge(ln[0]["lo"], B)
                    load(W1, ins["L0_ffn_w1"].rearrange("e d h -> d e h"), ffn_w_in)
                    load(W1 + 1024, ins["L0_ffn_sw1"], ffn_w_in)
                    load(W2, ins["L0_ffn_w2"].rearrange("e (c p) d -> p (e c) d", p=P), ffn_w_in)
                    load(W2 + 1024, ins["L0_ffn_sw2"].rearrange("(c p) d -> p c d", p=P), ffn_w_in)

            sp.wait_ge(far_in, 16)
            spread_q(0, 0)
            spread_k(0, 0)
            max_row_in(0, 0, 0)
            spread_q(1, 1)
            spread_k(1, 1)
            for k in range(1, 4):
                biases_out(k)
            attention(sp, iteration)

            with sp.Fori(0, B) as b:
                sp.wait_ge(y_done, b + 2)
                sp.dma_start(out_d[:, bass.ds(b * TPB, TPB), :],
                             x[:, bass.ds(b * S, S)].rearrange("p (t d) -> p t d", d=D)).then_inc(stored, 16)
            sp.wait_ge(stored, 16 * B)

        @block.gpsimd
        def _(pool):
            pool.dma_start(relT[:, :], ins["L0_attn_rel_emb"].rearrange("n h -> h n")).then_inc(rel_in, 16)
            pool.dma_start(buckets[:, :], consts["buckets"]).then_inc(buckets_in, 16)
            pool.memset(minus_half[:, :], -0.5).then_inc(halves, 1)
            pool.memset(v_hi[:, :], 1.0).then_inc(ones_in_v, 1)
            pool.wait_ge(halves, 1)

            def first_rstd(b):
                o = b * TPB
                pool.wait_ge(ln[0]["eps"], b + 1)
                pool.tensor_tensor(rstd[:, o:o + TPB], var_eps[:, o:o + TPB], minus_half[:, 0:TPB],
                                   ALU.pow).then_inc(ln[0]["rstd"], 1)

            def first_lo(b):
                pool.wait_ge(ln[0]["hi"], b + 1)
                pool.tensor_tensor(hT_lo[:, b * S:b * S + S], h32[0][:, (b % 2) * S:(b % 2) * S + S],
                                   hT_hi[:, b * S:b * S + S], ALU.subtract).then_inc(ln[0]["lo"], 1)

            def second_rstd(b, par):
                s = ln[1]
                o = par * TPB
                pool.wait_ge(s["eps"], b + 1)
                pool.tensor_tensor(rstd[:, o:o + TPB], var_eps[:, o:o + TPB], minus_half[:, 0:TPB],
                                   ALU.pow).then_inc(s["rstd"], 1)

            def second_lo(b):
                s = ln[1]
                pool.wait_ge(s["hi"], b + 1)
                at = bass.ds(b * S, S)
                pool.tensor_tensor(hT_lo[:, at], h32[1][:, :], hT_hi[:, at], ALU.subtract).then_inc(s["lo"], 1)

            first_rstd(0)
            pool.dma_start(b1T[:, 0:2 * HC].rearrange("p (e c) -> p e c", e=2),
                           ins["L0_ffn_b1"].rearrange("e (c p) -> p e c", p=P)).then_inc(ffn_small_in, 16)
            pool.dma_start(b1T[:, 2 * HC:3 * HC],
                           ins["L0_ffn_sb1"].rearrange("(c p) -> p c", p=P)).then_inc(ffn_small_in, 16)
            pool.dma_start(b2T[:, 0:2], ins["L0_ffn_b2"].rearrange("e p -> p e")).then_inc(ffn_small_in, 16)
            pool.dma_start(b2T[:, 2:3], ins["L0_ffn_sb2"].rearrange("(p o) -> p o", o=1)).then_inc(ffn_small_in, 16)
            pool.dma_start(gateT[:, :], ins["L0_ffn_gate_w"].rearrange("e p -> p e")).then_inc(ffn_small_in, 16)
            pool.memset(ones[:, :], 1.0).then_inc(ones_filled, 1)
            first_lo(0)
            first_rstd(1)
            first_rstd(2)
            first_lo(1)
            first_rstd(3)
            first_rstd(4)
            first_lo(2)
            first_rstd(5)
            first_lo(3)
            pool.wait_ge(bias_in, 16)

            def numerators(n, hh):
                g2 = ((n & (PAIRS - 1)) * 2 + hh) * BAND
                for kt in range(TPB):
                    q0, q1, c0 = band_of(kt)
                    o = (hh * TPB + kt) * S
                    pool.wait_ge(exp_done, 8 * n + 4 * hh + kt + 1)
                    at = ((g2 << kt) >> kt) + c0
                    pool.tensor_tensor(probs[:, o + q0:o + q1], probs[:, o + q0:o + q1],
                                       exp_bias[:, bass.ds(at, q1 - q0)], ALU.mult).then_inc(band_done, 1)
                for kt in POOL_LO[hh]:
                    o = (hh * TPB + kt) * S
                    pool.wait_ge(band_done, 8 * n + 4 * hh + kt + 1)
                    pool.tensor_tensor(probs_lo[:, o:o + S], probs[:, o:o + S],
                                       probs[:, o:o + S].bitcast(BF16)[:, 1:2 * S:2],
                                       ALU.subtract).then_inc(lo_pool, 1)

            def add_pairs(m):
                y = attn_T[:, bass.ds(((m >> 2) & (B - 1)) * S, S)]
                pool.wait_ge(wout_read, m + 2)
                pool.wait_ge(summed, m + 1)
                pool.tensor_tensor(y, y, attn_part[:, :], ALU.add).then_inc(summed, 1)

            def iteration(it, i):
                numerators(it, 0)
                if is_at(it, ITERS - 1):
                    second_rstd(0, 0)
                if is_at(it, 0) or is_at(it, 1):
                    first_lo(FIRST_LN + 2 * it)
                numerators(it, 1)
                if is_at(it, 0) or is_at(it, 1):
                    first_lo(FIRST_LN + 2 * it + 1)
                if is_at(it, 0):
                    first_rstd(6)
                    first_rstd(7)
                if is_at(it, 1):
                    pool.wait_ge(w_lo_done, ATTN_PIECES)
                    pool.memset(attn_T, 0.0).then_inc(summed, 1)
                if is_at(it, ITERS - 1):
                    second_lo(0)
                if i % 2 == 1 and not is_at(it, 1):
                    add_pairs(it // 2 - 1 if isinstance(it, int) else (it >> 1) - 1)
                if is_at(it, 1):
                    pool.wait_ge(bias_in, 16 * 4)

            attention(pool, iteration)
            add_pairs(ITERS // 2 - 1)

            def experts(b, par):
                if not is_at(b, B - 1):
                    second_rstd(b + 1, 1 - par)
                    second_lo(b + 1)

            batches(pool, experts)

        @block.scalar
        def _(act):
            act.dma_start(cT[:, 0:B], ins["L0_c"].rearrange("b d -> d b")).then_inc(c_in, 16)
            act.dma_start(tables[:, :], consts["tables"]).then_inc(tables_in, 16)
            act.dma_start(q_ext[DK:P, :].rearrange("p (s c) -> p s c", c=S),
                          consts["indicator"][DK:P, :].unsqueeze(1).to_broadcast([DK, 2 * RING, S])
                          ).then_inc(far_in, 16)
            act.wait_ge(c_in, 16)
            act.activation(cT[:, B:2 * B], cT[:, 0:B], ACT.Exp, scale=-1.0).then_inc(silu, 1)

            def weights_hi(k):
                o, n = w_pieces[k]
                done, count = w_piece_in[k]
                act.wait_ge(done, count)
                act.activation(w_part(w_hi, o, n), w_source(o, n), ACT.Copy).then_inc(w_hi_done, 1)

            def first_modulate(b):
                s = ln[0]
                o = (b % 2) * S
                act.wait_ge(s["xT"], b + 1)
                if b >= 2:
                    act.wait_ge(s["lo"], b - 1)
                act.activation(h32[0][:, o:o + S], ln_bank(b)[:, :], ACT.Identity,
                               bias=mod_col(0, b), scale=mod_col(1, b)).then_inc(s["h32"], 1)
                act.wait_ge(s["h32"], b + 1)
                act.activation(hT_hi[:, b * S:b * S + S], h32[0][:, o:o + S], ACT.Copy).then_inc(s["hi"], 1)

            def far_rows_of(g):
                o = g * 2 * S
                act.activation(k_lo[DK:P, o:o + 4 * S].rearrange("p (a c) -> p a c", c=P),
                               far_tile[DK:P, 2 * g * TPB:(2 * g + 4) * TPB].unsqueeze(2).to_broadcast(
                                   [DK, 4 * TPB, P]), ACT.Copy).then_inc(far_rows, 1)

            def modulate(b):
                s = ln[1]
                act.wait_ge(s["xT"], b + 1)
                if not is_at(b, 0):
                    act.wait_ge(s["lo"], b)
                act.activation(h32[1][:, :], PROJ[:, :], ACT.Identity,
                               bias=mod_col(3, b), scale=mod_col(4, b)).then_inc(s["h32"], 1)

            def modulated_hi(b):
                s = ln[1]
                act.wait_ge(s["h32"], b + 1)
                act.activation(hT_hi[:, bass.ds(b * S, S)], h32[1][:, :], ACT.Copy).then_inc(s["hi"], 1)

            def back_copy(b):
                act.wait_ge(summed, 1 + (b + 1) * (PAIRS // 2))
                if is_at(b, 1):
                    act.wait_ge(wo_done, ITERS)
                else:
                    act.wait_ge(attn_back, b)
                act.activation(back_T[:, :], attn_T[:, bass.ds(b * S, S)], ACT.Copy).then_inc(back_in, 1)

            weights_hi(0)
            act.wait_ge(rel_mm, 1)
            act.activation(eb_row[:, :], TURN[0:H, 0:OFFS], ACT.Exp).then_inc(bias_row, 1)
            weights_hi(1)
            act.wait_ge(mod_mm, 1)
            act.activation(mod[:, :], PROJ[:, 0:6 * B], ACT.Copy).then_inc(mod_out, 1)
            weights_hi(2)
            act.wait_ge(mod_ready, 1)
            first_modulate(0)

            def exponentials(n, hh, kts):
                for kt in kts:
                    if kt == 0 and not (isinstance(n, int) and n == 0):
                        act.wait_ge(pv_done, 2 * n - 1 + hh)
                    o = (hh * TPB + kt) * S
                    act.wait_ge(scores_done, 8 * n + 4 * hh + kt + 1)
                    act.activation(probs[:, o:o + S], st_bank(kt)[:, :], ACT.Exp).then_inc(exp_done, 1)

            def pair_hi_part(n, k):
                act.wait_ge(proj_done, 3 * n + k + 1)
                if not (isinstance(n, int) and n == 0):
                    act.wait_ge(spread_a, 64 * n)
                    act.wait_ge(spread_b, 32 * n)
                act.activation(pair_hi[:, k * S:k * S + S], PROJ[:, :], ACT.Copy).then_inc(qkv_hi, 1)

            def v_hi_part(n, ring):
                act.wait_ge(proj_done, 3 * n + 3)
                o = ring * 2 * TPB * VP
                act.activation(v_hi[:, o:o + 2 * TPB * VP].rearrange("p (a c) -> p a c", c=VP)[:, :, 0:DK],
                               PROJ[:, :].rearrange("p (a c) -> p a c", c=DK), ACT.Copy).then_inc(qkv_hi, 1)

            def max_row_out(n, hh):
                act.wait_ge(topT_done, 2 * n + hh + 1)
                if not (isinstance(n, int) and n == 0):
                    act.wait_ge(mrow_in[hh], 16 * n)
                act.activation(max_row[:, hh * P:hh * P + P], TURN[0:TPB, 0:P], ACT.Copy,
                               scale=-1.0 / M_SCALE).then_inc(mrow_done, 1)

            def context_out(n):
                act.wait_ge(ctxT_done, n + 1)
                act.activation(ctxT[:, :], TURN[:, :], ACT.Copy).then_inc(ctx_out, 1)

            def attn_part_out(m):
                act.wait_ge(wo_done, 2 * m + 2)
                act.wait_ge(summed, m + 1)
                act.activation(attn_part[:, :], WOUT[:, :], ACT.Copy,
                               scale=gates[:, bass.ds((m >> 2) & (B - 1), 1)]).then_inc(wout_read, 1)

            def iteration(it, i):
                project, rate = not is_at(it, ITERS - 2) and not is_at(it, ITERS - 1), not is_at(it, ITERS - 1)
                exponentials(it, 0, (0, 1))
                if project:
                    pair_hi_part(it + 2, 0)
                else:
                    weights_hi(7 if rate else 9)
                exponentials(it, 0, (2, 3))
                max_row_out(it, 1)
                if is_at(it, 0) or is_at(it, 1):
                    first_modulate(FIRST_LN + 2 * it)
                if project:
                    pair_hi_part(it + 2, 1)
                else:
                    weights_hi(8 if rate else 10)
                exponentials(it, 1, (0, 1))
                exponentials(it, 1, (2, 3))
                if i % 2 == 1 and not is_at(it, 1):
                    attn_part_out(it // 2 - 1 if isinstance(it, int) else (it >> 1) - 1)
                if rate:
                    max_row_out(it + 1, 0)
                else:
                    modulate(0)
                    modulated_hi(0)
                if project:
                    v_hi_part(it + 2, (i + 2) % RING)
                if not is_at(it, 0):
                    context_out(it - 1)
                if is_at(it, 0) or is_at(it, 1):
                    first_modulate(FIRST_LN + 2 * it + 1)
                    far_rows_of(4 + 2 * it)
                if is_at(it, 1):
                    act.wait_ge(gates_ready, 1)

            pair_hi_part(0, 0)
            weights_hi(3)
            pair_hi_part(0, 1)
            weights_hi(4)
            act.wait_ge(ones_in_v, 1)
            v_hi_part(0, 0)
            first_modulate(1)
            pair_hi_part(1, 0)
            act.wait_ge(far_step, 5)
            far_rows_of(0)
            weights_hi(5)
            pair_hi_part(1, 1)
            max_row_out(0, 0)
            first_modulate(2)
            v_hi_part(1, 1)
            weights_hi(6)
            first_modulate(3)
            far_rows_of(2)
            attention(act, iteration)

            def experts(b, par):
                for c in range(CHUNKS):
                    if c == 1 and is_at(b, 0):
                        context_out(ITERS - 1)
                    if c == 3 and is_at(b, 0):
                        attn_part_out(ITERS // 2 - 1)
                    if c == 3 and not is_at(b, B - 1):
                        back_copy(b + 1)
                    if c == 10 and not is_at(b, B - 1):
                        modulate(b + 1)
                    if c == 11 and not is_at(b, B - 1):
                        modulated_hi(b + 1)
                    e = (2, 0, 1)[c // HC]
                    act.wait_ge(up_done, CHUNKS * b + c + 1)
                    if c >= 4:
                        act.wait_ge(down_done, CHUNKS * b + c - 3)
                    elif is_at(b, 0):
                        act.wait_ge(pv_done, 2 * ITERS - 1)
                    else:
                        act.wait_ge(down_done, CHUNKS * b)
                    act.activation(hid[:, (c % 4) * S:(c % 4) * S + S], bank[c % 2][:, :], ACT.Relu,
                                   bias=b1T[:, e * HC + c % HC:e * HC + c % HC + 1]).then_inc(hid_done, 1)
                act.wait_ge(down_done, CHUNKS * b + CHUNKS)
                if not is_at(b, 0):
                    act.wait_ge(moe_back, b)
                act.activation(moe_T[:, :], bank[2][:, :], ACT.Identity, bias=b2g[:, bass.ds(b, 1)],
                               scale=gates[:, bass.ds(4 * B + b, 1)]).then_inc(moe_done, 1)

            act.wait_ge(ffn_small_in, 16 * 5)
            act.wait_ge(ffn_ready, 1)
            batches(act, experts)

        @block.vector
        def _(dve):
            def first_stats(b):
                s = ln[0]
                for n in range(b * TPB, b * TPB + TPB):
                    dve.bn_stats(stats[:, 6 * n:6 * n + 6], x[:, n * P:n * P + P]).then_inc(s["stats"], 1)
                dve.wait_ge(s["stats"], (b + 1) * TPB)
                for n in range(b * TPB, b * TPB + TPB):
                    dve.bn_aggr(mean_var[:, 2 * n:2 * n + 2], stats[:, 6 * n:6 * n + 6]).then_inc(s["aggr"], 1)
                dve.wait_ge(s["aggr"], (b + 1) * TPB)
                o = b * TPB
                dve.tensor_scalar(var_eps[:, o:o + TPB], mean_var[:, 2 * o + 1:2 * (o + TPB):2], EPS, None,
                                  ALU.add).then_inc(s["eps"], 1)

            def first_rows(b):
                s = ln[0]
                dve.wait_ge(s["rstd"], b + 1)
                if b >= 2:
                    dve.wait_ge(s["xT"], b - 1)
                for t in range(TPB):
                    n = b * TPB + t
                    o = (b % 2) * S + t * P
                    dve.tensor_scalar(xn[0][:, o:o + P], x[:, n * P:n * P + P], mean_var[:, 2 * n:2 * n + 1],
                                      rstd[:, n:n + 1], ALU.subtract, ALU.mult).then_inc(s["xn"], 1)

            def weights_lo(k):
                o, n = w_pieces[k]
                dve.wait_ge(w_hi_done, k + 1)
                dve.tensor_tensor(w_part(w_lo, o, n), w_source(o, n), w_part(w_hi, o, n),
                                  ALU.subtract).then_inc(w_lo_done, 1)

            def far_constants():
                dve.wait_ge(tables_in, 16)
                dve.wait_ge(rel_mm, 2)
                dve.tensor_copy(far[:, 0:H], WOUT[:, 0:H]).then_inc(far_step, 1)
                dve.wait_ge(far_step, 1)
                dve.tensor_copy(far_hi[:, :], far[:, 0:H]).then_inc(far_step, 1)
                dve.wait_ge(far_step, 2)
                dve.tensor_tensor(far[:, H:2 * H], far[:, 0:H], far_hi[:, :], ALU.subtract).then_inc(wout_read, 1)
                dve.tensor_scalar(far[:, 2 * H:3 * H], far_hi[:, :], rowmask[:, 0:1], rowmask[:, 2:3],
                                  ALU.mult, ALU.add).then_inc(far_step, 1)
                dve.wait_ge(far_step, 3)
                dve.scalar_tensor_tensor(far[:, 0:H], far[:, H:2 * H], rowmask[:, 1:2], far[:, 2 * H:3 * H],
                                         ALU.mult, ALU.add).then_inc(far_step, 1)
                dve.wait_ge(far_step, 4)
                dve.tensor_tensor(far_tile[:, :].rearrange("p (h j) -> p h j", j=TPB),
                                  far[:, 0:H].unsqueeze(2).to_broadcast([P, H, TPB]),
                                  rowmask[:, 3:3 + TPB].unsqueeze(1).to_broadcast([P, H, TPB]),
                                  ALU.mult).then_inc(far_step, 1)

            def gates_from_mod():
                for k, i in enumerate((2, 5)):
                    raw = mod[:, i * B:i * B + B]
                    o = k * 4 * B
                    dve.tensor_scalar(gates[:, o + B:o + 2 * B], raw, -1.0, None, ALU.mult)
                    dve.tensor_scalar(gates[:, o + 2 * B:o + 3 * B], raw, 0.0, 2.0, ALU.is_ge, ALU.mult)
                    dve.drain()
                    dve.tensor_tensor(gates[:, o + B:o + 2 * B], gates[:, o + B:o + 2 * B], raw, ALU.max)
                    dve.tensor_scalar(gates[:, o + 2 * B:o + 3 * B], gates[:, o + 2 * B:o + 3 * B], -1.0, None,
                                      ALU.add)
                    dve.drain()
                    dve.tensor_scalar(gates[:, o + B:o + 2 * B], gates[:, o + B:o + 2 * B], 0.25, None, ALU.max)
                    dve.drain()
                    last = dve.tensor_tensor(gates[:, o:o + B], gates[:, o + B:o + 2 * B],
                                             gates[:, o + 2 * B:o + 3 * B], ALU.mult)
                last.then_inc(gates_ready, 1)

            def expert_constants():
                gate32 = wmod[:, 0:2 * P]
                dve.wait_ge(ones_filled, 1)
                dve.wait_ge(ffn_small_in, 16 * 5)
                for e in range(2):
                    sign = -1.0 if e == 0 else 1.0
                    dve.tensor_scalar(gate32[:, e * P:e * P + P], ones[:, :], gateT[:, e:e + 1], sign, ALU.mult,
                                      ALU.mult)
                dve.drain()
                dve.tensor_copy(gate_hi[:, :], gate32).then_inc(y_done, 1)
                dve.drain()
                dve.tensor_tensor(gate_lo[:, :], gate32, gate_hi[:, :], ALU.subtract)
                dve.tensor_tensor(b2T[:, 3:4], b2T[:, 0:1], b2T[:, 1:2], ALU.add)
                dve.drain()
                dve.tensor_tensor(b2T[:, 4:5], b2T[:, 3:4], b2T[:, 2:3], ALU.add)
                dve.drain()
                dve.tensor_scalar(b2g[:, :], gates[:, 4 * B:5 * B], b2T[:, 4:5], None, ALU.mult).then_inc(ffn_ready, 1)

            dve.wait_ge(x0_in, 16)
            first_stats(0)
            dve.wait_ge(rel_in, 16)
            dve.reduce_max(rel_top[:, :], relT[:, :], AXX).then_inc(rel_step, 1)
            dve.wait_ge(rel_step, 1)
            dve.tensor_scalar(relT[:, :], relT[:, :], rel_top[:, 0:1], None, ALU.subtract).then_inc(rel_step, 1)
            dve.wait_ge(silu, 1)
            dve.tensor_scalar(cT[:, B:2 * B], cT[:, B:2 * B], 1.0, None, ALU.add).then_inc(silu, 1)
            dve.wait_ge(silu, 2)
            dve.reciprocal(cT[:, 2 * B:3 * B], cT[:, B:2 * B]).then_inc(silu, 1)
            dve.wait_ge(silu, 3)
            dve.tensor_tensor(cT[:, B:2 * B], cT[:, 0:B], cT[:, 2 * B:3 * B], ALU.mult).then_inc(silu, 1)
            dve.wait_ge(rel_turned, 1)
            dve.tensor_copy(rel[:, :], WOUT[0:BUCKETS, 0:H]).then_inc(rel_step, 1)
            first_rows(0)
            weights_lo(0)
            weights_lo(1)
            dve.wait_ge(mod_out, 1)
            dve.tensor_scalar(mod[:, B:2 * B], mod[:, B:2 * B], 1.0, None, ALU.add).then_inc(mod_ready, 1)
            dve.tensor_scalar(mod[:, 4 * B:5 * B], mod[:, 4 * B:5 * B], 1.0, None, ALU.add).then_inc(mod_ready, 1)
            weights_lo(2)

            def add_attention(b):
                dve.wait_ge(attn_back, b + 1)
                xb = x[:, bass.ds(b * S, S)]
                dve.tensor_tensor(xb, xb, PROJ[:, :], ALU.add).then_inc(resid, 1)

            def row_stats(b, par):
                for t in range(TPB):
                    o = (par * TPB + t) * 6
                    dve.bn_stats(stats[:, o:o + 6], x[:, bass.ds(b * S + t * P, P)]).then_inc(ln[1]["stats"], 1)

            def variances(b, par):
                s = ln[1]
                for t in range(TPB):
                    n = par * TPB + t
                    dve.bn_aggr(mean_var[:, 2 * n:2 * n + 2], stats[:, 6 * n:6 * n + 6]).then_inc(s["aggr"], 1)
                dve.wait_ge(s["aggr"], (b + 1) * TPB)
                o = par * TPB
                dve.tensor_scalar(var_eps[:, o:o + TPB], mean_var[:, 2 * o + 1:2 * (o + TPB):2], EPS, None,
                                  ALU.add).then_inc(s["eps"], 1)

            def normalise_rows(b, par):
                dve.wait_ge(ln[1]["rstd"], b + 1)
                for t in range(TPB):
                    n = par * TPB + t
                    dve.tensor_scalar(xn[1][:, t * P:t * P + P], x[:, bass.ds(b * S + t * P, P)],
                                      mean_var[:, 2 * n:2 * n + 1], rstd[:, n:n + 1], ALU.subtract,
                                      ALU.mult).then_inc(ln[1]["xn"], 1)

            def top(n, hh, t):
                if t == 0 and not (isinstance(n, int) and n == 0):
                    dve.wait_ge(topT_done, 2 * n - 1 + hh)
                dve.wait_ge(tops_done, 8 * n + 4 * hh + t + 1)
                dve.reduce_max(row_max[:, hh * TPB + t:hh * TPB + t + 1], s_bank(t)[:, :], AXX).then_inc(top_done, 1)

            def lo(n, hh, kt):
                o = (hh * TPB + kt) * S
                dve.wait_ge(band_done, 8 * n + 4 * hh + kt + 1)
                dve.tensor_tensor(probs_lo[:, o:o + S], probs[:, o:o + S],
                                  probs[:, o:o + S].bitcast(BF16)[:, 1:2 * S:2], ALU.subtract).then_inc(lo_dve, 1)

            def context_lo(n):
                dve.wait_ge(ctx_out, n + 1)
                dve.tensor_tensor(ctxT_lo[:, :], ctxT[:, :], ctxT[:, :].bitcast(BF16)[:, 1:2 * S:2],
                                   ALU.subtract).then_inc(ctx_lo, 1)

            def pair_lo_part(n, k):
                dve.wait_ge(qkv_hi, 3 * n + k + 1)
                dve.tensor_tensor(pair_lo[:, k * S:k * S + S], PROJ[:, :], pair_hi[:, k * S:k * S + S],
                                  ALU.subtract).then_inc(qkv_lo, 1)

            def v_lo_part(n, ring):
                dve.wait_ge(qkv_hi, 3 * n + 3)
                o, ol = ring * 2 * TPB * VP, ring * 2 * TPB * DK
                dve.tensor_tensor(v_lo[:, ol:ol + 2 * TPB * DK].rearrange("p (a c) -> p a c", c=DK),
                                  PROJ[:, :].rearrange("p (a c) -> p a c", c=DK),
                                  v_hi[:, o:o + 2 * TPB * VP].rearrange("p (a c) -> p a c", c=VP)[:, :, 0:DK],
                                  ALU.subtract).then_inc(qkv_lo, 1)

            pvv = PV[:, 0:TPB * (DK + 1)].rearrange("p (t c) -> p t c", c=DK + 1)

            def reciprocals(n, hh):
                dve.wait_ge(pv_done, 2 * n + hh + 1)
                dve.reciprocal(recip[:, :].unsqueeze(2), pvv[:, :, DK:DK + 1]).then_inc(recip_done, 1)

            def normalise(n, hh):
                dve.wait_ge(recip_done, 2 * n + hh + 1)
                if hh == 0 and not is_at(n, 0):
                    dve.wait_ge(ctxT_done, n)
                dve.tensor_tensor(ctx_n[:, :].rearrange("p (t c) -> p t c", c=P)[:, :, hh * DK:hh * DK + DK],
                                  pvv[:, :, 0:DK], recip[:, :].unsqueeze(2).to_broadcast([P, TPB, DK]),
                                  ALU.mult).then_inc(norm_done, 1)

            def iteration(it, i):
                project, rate = not is_at(it, ITERS - 2) and not is_at(it, ITERS - 1), not is_at(it, ITERS - 1)
                top(it, 1, 0)
                if rate:
                    v_lo_part(it + 1, (i + 1) % RING)
                top(it, 1, 1)
                if is_at(it, 0) or is_at(it, 1):
                    first_rows(FIRST_LN + 2 * it)
                if is_at(it, 0):
                    first_stats(6)
                    first_stats(7)
                top(it, 1, 2)
                if not is_at(it, 0):
                    reciprocals(it - 1, 0)
                top(it, 1, 3)
                if not is_at(it, 0):
                    normalise(it - 1, 0)
                if not is_at(it, 0) and not is_at(it, 1):
                    context_lo(it - 2)
                if not rate:
                    add_attention(0)
                    dve.wait_ge(resid, 1)
                    row_stats(0, 0)
                    dve.wait_ge(ln[1]["stats"], TPB)
                    variances(0, 0)
                if project:
                    pair_lo_part(it + 2, 0)
                elif rate:
                    weights_lo(7)
                for kt in DVE_LO[0]:
                    lo(it, 0, kt)
                if not rate:
                    normalise_rows(0, 0)
                if rate:
                    top(it + 1, 0, 0)
                    top(it + 1, 0, 1)
                if project:
                    pair_lo_part(it + 2, 1)
                elif rate:
                    expert_constants()
                else:
                    for k in (8, 9, 10):
                        weights_lo(k)
                if is_at(it, 0):
                    weights_lo(6)
                if is_at(it, 1):
                    gates_from_mod()
                if is_at(it, 0) or is_at(it, 1):
                    first_rows(FIRST_LN + 2 * it + 1)
                if rate:
                    top(it + 1, 0, 2)
                if not is_at(it, 0):
                    reciprocals(it - 1, 1)
                if rate:
                    top(it + 1, 0, 3)
                if not is_at(it, 0):
                    normalise(it - 1, 1)
                for kt in DVE_LO[1]:
                    lo(it, 1, kt)

            far_constants()
            pair_lo_part(0, 0)
            dve.wait_ge(x_in, 16)
            first_stats(1)
            pair_lo_part(0, 1)
            first_stats(2)
            v_lo_part(0, 0)
            weights_lo(3)
            first_rows(1)
            weights_lo(4)
            top(0, 0, 0)
            top(0, 0, 1)
            pair_lo_part(1, 0)
            top(0, 0, 2)
            top(0, 0, 3)
            first_stats(3)
            first_rows(2)
            pair_lo_part(1, 1)
            first_stats(4)
            first_rows(3)
            weights_lo(5)
            first_stats(5)
            attention(dve, iteration)
            reciprocals(ITERS - 1, 0)
            normalise(ITERS - 1, 0)
            context_lo(ITERS - 2)
            reciprocals(ITERS - 1, 1)
            normalise(ITERS - 1, 1)

            def mask(b, e, k):
                dve.wait_ge(gate_done, b + 1)
                o = (2 * e + k) * S
                src = (hT_hi, hT_lo)[k]
                dve.scalar_tensor_tensor(xm[:, o:o + S], bank[3][:, :], 0.0, src[:, bass.ds(b * S, S)],
                                         ALU.is_gt if e == 1 else ALU.is_le, ALU.mult).then_inc(masked, 1)

            def block_output(b):
                dve.wait_ge(moe_back, b + 1)
                xb = x[:, bass.ds(b * S, S)]
                dve.tensor_tensor(xb, xb, bank[4][:, :], ALU.add).then_inc(y_done, 1)

            def experts(b, par):
                more = not is_at(b, B - 1)
                for c in range(CHUNKS):
                    o = (c % 4) * S
                    if c == 5 and more:
                        dve.wait_ge(resid, b + 2)
                    if c == 6 and more:
                        dve.wait_ge(ln[1]["stats"], (b + 2) * TPB)
                    dve.wait_ge(hid_done, CHUNKS * b + c + 1)
                    dve.tensor_tensor(hid_lo[:, o:o + S], hid[:, o:o + S],
                                      hid[:, o:o + S].bitcast(BF16)[:, 1:2 * S:2],
                                      ALU.subtract).then_inc(hid_lo_done, 1)
                    if c == 0 and is_at(b, 0):
                        context_lo(ITERS - 1)
                    if c < 4:
                        mask(b, c // 2, c % 2)
                    if c == 9 and not is_at(b, 0):
                        block_output(b - 1)
                    if c == 4 and more:
                        add_attention(b + 1)
                    if c == 5 and more:
                        row_stats(b + 1, 1 - par)
                    if c == 6 and more:
                        variances(b + 1, 1 - par)
                    if c == 7 and more:
                        normalise_rows(b + 1, 1 - par)

            batches(dve, experts)
            block_output(B - 1)

        @block.tensor
        def _(pe):
            pe.wait_ge(tables_in, 16)
            pe.wait_ge(rel_step, 2)
            pe.transpose(WOUT[0:BUCKETS, 0:H], relT[:, :], ident[0:H, 0:H]).then_inc(rel_turned, 1)
            pe.wait_ge(buckets_in, 16)
            pe.wait_ge(rel_step, 3)
            pe.matmul(TURN[0:H, 0:OFFS], rel[:, :], onehot, start=True, stop=True).then_inc(rel_mm, 1)
            pe.matmul(WOUT[:, 0:H], select, rel[:, :], start=True, stop=True).then_inc(rel_mm, 1)
            pe.wait_ge(wmod_in, 16)
            pe.wait_ge(silu, 4)
            for i in range(6):
                mm = pe.matmul(PROJ[:, i * B:i * B + B], wmod[:, i * D:i * D + D], cT[:, B:2 * B],
                               start=True, stop=True)
            mm.then_inc(mod_mm, 1)

            def first_turn(b):
                s = ln[0]
                if b == FIRST_LN:
                    pe.wait_ge(wout_read, 1)
                elif b > FIRST_LN:
                    pe.wait_ge(s["h32"], b)
                elif b >= 2:
                    pe.wait_ge(s["h32"], b - 1)
                pe.wait_ge(s["xn"], TPB * (b + 1))
                for t in range(TPB):
                    o = (b % 2) * S + t * P
                    mm = pe.transpose(ln_bank(b)[:, t * P:t * P + P], xn[0][:, o:o + P], ident)
                mm.then_inc(s["xT"], 1)

            def turn_back(b, src):
                for t in range(TPB):
                    mm = pe.transpose(PROJ[:, t * P:t * P + P], src[:, t * P:t * P + P], ident)
                mm.then_inc(attn_back, 1)

            def turn_rows(b):
                pe.wait_ge(resid, b + 1)
                pe.wait_ge(ln[1]["xn"], TPB * b + TPB)
                for t in range(TPB):
                    mm = pe.transpose(PROJ[:, t * P:t * P + P], xn[1][:, t * P:t * P + P], ident)
                mm.then_inc(ln[1]["xT"], 1)

            first_turn(0)

            def q_or_k(n, w, count):
                b, g = (n >> 3) & (B - 1), n & (PAIRS - 1)
                if not (isinstance(n, int) and n == 0 and count == 0):
                    pe.wait_ge(qkv_lo, 3 * n + count)
                h_hi, h_lo = hT_hi[:, bass.ds(b * S, S)], hT_lo[:, bass.ds(b * S, S)]
                pe.matmul(PROJ[:, :], w_hi[:, bass.ds(w + g * P, P)], h_hi, start=True, stop=False)
                pe.matmul(PROJ[:, :], w_lo[:, bass.ds(w + g * P, P)], h_hi, start=False, stop=False)
                pe.matmul(PROJ[:, :], w_hi[:, bass.ds(w + g * P, P)], h_lo, start=False,
                          stop=True).then_inc(proj_done, 1)

            def v_proj(n, tiles=range(TPB)):
                b, g = (n >> 3) & (B - 1), n & (PAIRS - 1)
                if 0 in tiles:
                    pe.wait_ge(qkv_lo, 3 * n + 2)
                wv_hi, wv_lo = w_hi[:, bass.ds(WV + g * P, P)], w_lo[:, bass.ds(WV + g * P, P)]
                rows_hi, rows_lo = hT_hi[:, bass.ds(b * S, S)], hT_lo[:, bass.ds(b * S, S)]
                for t in tiles:
                    o = PROJ[:, t * P:t * P + P]
                    h_hi, h_lo = rows_hi[:, t * P:t * P + P], rows_lo[:, t * P:t * P + P]
                    pe.matmul(o, h_hi, wv_hi, start=True, stop=False)
                    pe.matmul(o, h_hi, wv_lo, start=False, stop=False)
                    mm = pe.matmul(o, h_lo, wv_hi, start=False, stop=True)
                if TPB - 1 in tiles:
                    mm.then_inc(proj_done, 1)

            def rough_scores(n, ring, hh, t):
                idx = 8 * n + 4 * hh + t
                o = slot(ring, hh)
                if not (isinstance(n, int) and n == 0) or hh or t >= 2:
                    pe.wait_ge(top_done, idx - 1)
                if hh == 0 and t == 0:
                    pe.wait_ge(spread_a, 64 * n + 64)
                pe.matmul(s_bank(t)[:, :], q_hilo[:, o + t * P:o + t * P + P], k_hihi[:, o:o + S],
                          start=True, stop=True).then_inc(tops_done, 1)

            def scores(n, ring, hh, kt):
                idx = 8 * n + 4 * hh + kt
                o = slot(ring, hh)
                if not (isinstance(n, int) and n == 0) or hh or kt >= 2:
                    pe.wait_ge(exp_done, idx - 1)
                pe.matmul(st_bank(kt)[:, :], k_hihi[:, o + kt * P:o + kt * P + P], q_hilo[:, o:o + S],
                          start=True, stop=False)
                if kt == 0:
                    pe.wait_ge(mrow_in[hh], 16 * n + 16)
                    if hh == 0:
                        pe.wait_ge(spread_b, 32 * n + 32)
                pe.matmul(st_bank(kt)[:, :],
                          k_lo[:, bass.ds(((n & (PAIRS - 1)) * 2 + hh) * S + kt * P, P)],
                          q_ext[:, o:o + S], start=False, stop=True).then_inc(scores_done, 1)

            def turn_tops(n, hh):
                pe.wait_ge(top_done, 8 * n + 4 * hh + 4)
                if hh == 0:
                    if not is_at(n, 0):
                        pe.wait_ge(mrow_done, 2 * n)
                elif not isinstance(n, int) or n > 1:
                    pe.wait_ge(ctx_out, n - 1)
                else:
                    pe.wait_ge(mrow_done, 2 * n + 1)
                pe.transpose(TURN[0:TPB, 0:P], row_max[:, hh * TPB:hh * TPB + TPB], ident).then_inc(topT_done, 1)

            def attend(n, ring, hh):
                pe.wait_ge(lo_dve, lo_count(DVE_LO, n, hh))
                pe.wait_ge(lo_pool, lo_count(POOL_LO, n, hh))
                pe.wait_ge(qkv_lo, 3 * n + 3)
                if not (is_at(n, 0) and hh == 0):
                    pe.wait_ge(norm_done, 2 * n + hh)
                for t in range(TPB):
                    o = t * (DK + 1)
                    for kt in range(TPB):
                        a = (ring * TPB + kt) * 2 + hh
                        vh, vl = v_hi[:, a * VP:a * VP + DK + 1], v_lo[:, a * DK:a * DK + DK]
                        pcol = (hh * TPB + kt) * S + t * P
                        p_hi = probs[:, pcol:pcol + P].bitcast(BF16)[:, 1:2 * P:2]
                        pe.matmul(PV[:, o:o + DK + 1], p_hi, vh, start=kt == 0, stop=False)
                        pe.matmul(PV[:, o:o + DK], p_hi, vl, start=False, stop=False)
                        mm = pe.matmul(PV[:, o:o + DK + 1], probs_lo[:, pcol:pcol + P], vh, start=False,
                                       stop=kt == TPB - 1)
                mm.then_inc(pv_done, 1)

            def turn_context(n):
                pe.wait_ge(norm_done, 2 * n + 2)
                if is_at(n, ITERS - 1):
                    pe.wait_ge(ctx_out, ITERS - 1)
                elif is_at(n, ITERS - 2):
                    pe.wait_ge(mrow_done, 2 * ITERS)
                else:
                    pe.wait_ge(mrow_done, 2 * n + 5)
                for t in range(TPB):
                    mm = pe.transpose(TURN[:, t * P:t * P + P], ctx_n[:, t * P:t * P + P], ident)
                mm.then_inc(ctxT_done, 1)

            def out_product(n, odd):
                g = n & (PAIRS - 1)
                c_hi = ctxT[:, :].bitcast(BF16)[:, 1:2 * S:2]
                pe.wait_ge(ctx_lo, n + 1)
                if not odd:
                    pe.wait_ge(wout_read, (n >> 1) + 1)
                pe.matmul(WOUT[:, :], w_hi[:, bass.ds(WO + g * P, P)], c_hi, start=not odd, stop=False)
                pe.matmul(WOUT[:, :], w_lo[:, bass.ds(WO + g * P, P)], c_hi, start=False, stop=False)
                pe.matmul(WOUT[:, :], w_hi[:, bass.ds(WO + g * P, P)], ctxT_lo[:, :], start=False,
                          stop=odd).then_inc(wo_done, 1)

            def iteration(it, i):
                ring, nxt, nring = i % RING, it + 1, (i + 1) % RING
                after, last = not is_at(it, 0), is_at(it, ITERS - 1)
                project, rate = not last and not is_at(it, ITERS - 2), not last
                rough_scores(it, ring, 1, 2)
                scores(it, ring, 0, 0)
                rough_scores(it, ring, 1, 3)
                scores(it, ring, 0, 1)
                if project:
                    q_or_k(it + 2, WQ, 0)
                if last:
                    pe.wait_ge(summed, 1 + PAIRS // 2)
                    turn_back(0, attn_T[:, 0:S])
                scores(it, ring, 0, 2)
                scores(it, ring, 0, 3)
                turn_tops(it, 1)
                if is_at(it, 0) or is_at(it, 1):
                    first_turn(FIRST_LN + 2 * it)
                if rate:
                    rough_scores(nxt, nring, 0, 0)
                    rough_scores(nxt, nring, 0, 1)
                if after:
                    attend(it - 1, (i - 1) % RING, 1)
                if project:
                    q_or_k(it + 2, WK, 1)
                if after and not is_at(it, 1):
                    out_product(it - 2, odd=i % 2 == 1)
                if rate:
                    rough_scores(nxt, nring, 0, 2)
                scores(it, ring, 1, 0)
                scores(it, ring, 1, 1)
                if rate:
                    rough_scores(nxt, nring, 0, 3)
                scores(it, ring, 1, 2)
                scores(it, ring, 1, 3)
                if project:
                    v_proj(it + 2, (0, 1))
                if rate:
                    turn_tops(nxt, 0)
                    rough_scores(nxt, nring, 1, 0)
                    rough_scores(nxt, nring, 1, 1)
                if project:
                    v_proj(it + 2, (2, 3))
                if last:
                    turn_rows(0)
                attend(it, ring, 0)
                if after:
                    turn_context(it - 1)
                if is_at(it, 0) or is_at(it, 1):
                    first_turn(FIRST_LN + 2 * it + 1)
                if is_at(it, 1):
                    pe.wait_ge(ln[0]["h32"], B)
                    pe.wait_ge(w_lo_done, ATTN_PIECES)
                    pe.wait_ge(far_rows, 4)
                if i == 2:
                    pe.wait_ge(ln[0]["lo"], B)

            pe.wait_ge(ln[0]["lo"], 1)
            pe.wait_ge(mod_out, 1)
            pe.wait_ge(w_lo_done, 2)
            q_or_k(0, WQ, 0)
            q_or_k(0, WK, 1)
            pe.wait_ge(w_lo_done, 3)
            v_proj(0)
            q_or_k(1, WQ, 0)
            first_turn(1)
            rough_scores(0, 0, 0, 0)
            rough_scores(0, 0, 0, 1)
            rough_scores(0, 0, 0, 2)
            rough_scores(0, 0, 0, 3)
            q_or_k(1, WK, 1)
            pe.wait_ge(bias_row, 1)
            turn_tops(0, 0)
            first_turn(2)
            v_proj(1)
            rough_scores(0, 0, 1, 0)
            rough_scores(0, 0, 1, 1)
            first_turn(3)
            pe.wait_ge(ln[0]["h32"], FIRST_LN)
            pe.wait_ge(w_lo_done, 6)
            pe.wait_ge(far_in, 16)
            pe.wait_ge(far_rows, 1)
            attention(pe, iteration)

            def up(b, c):
                e = (2, 0, 1)[c // HC]
                w = W1 + e * HID + (c % HC) * P
                if e == 2:
                    x_hi, x_lo = hT_hi[:, bass.ds(b * S, S)], hT_lo[:, bass.ds(b * S, S)]
                else:
                    x_hi, x_lo = xm[:, 2 * e * S:2 * e * S + S], xm[:, (2 * e + 1) * S:(2 * e + 2) * S]
                    if c % HC == 0:
                        pe.wait_ge(masked, 4 * b + 2 * e + 2)
                hb = bank[c % 2]
                if c >= 2:
                    pe.wait_ge(hid_done, CHUNKS * b + c - 1)
                elif is_at(b, 0):
                    pe.wait_ge(exp_done, 8 * ITERS)
                else:
                    pe.wait_ge(hid_done, CHUNKS * b)
                pe.matmul(hb[:, :], w_hi[:, w:w + P], x_hi, start=True, stop=False)
                pe.matmul(hb[:, :], w_lo[:, w:w + P], x_hi, start=False, stop=False)
                pe.matmul(hb[:, :], w_hi[:, w:w + P], x_lo, start=False, stop=True).then_inc(up_done, 1)

            def down(b, c):
                e = (2, 0, 1)[c // HC]
                w = W2 + (e * HC + c % HC) * D
                o = (c % 4) * S
                h_hi = hid[:, o:o + S].bitcast(BF16)[:, 1:2 * S:2]
                pe.wait_ge(hid_lo_done, CHUNKS * b + c + 1)
                if c == 0 and not is_at(b, 0):
                    pe.wait_ge(moe_done, b)
                pe.matmul(bank[2][:, :], w_hi[:, w:w + P], h_hi, start=c == 0, stop=False)
                pe.matmul(bank[2][:, :], w_lo[:, w:w + P], h_hi, start=False, stop=False)
                pe.matmul(bank[2][:, :], w_hi[:, w:w + P], hid_lo[:, o:o + S], start=False,
                          stop=c == CHUNKS - 1).then_inc(down_done, 1)

            def gate(b):
                pe.wait_ge(ln[1]["lo"], b + 1)
                if not is_at(b, 0):
                    pe.wait_ge(masked, 4 * b)
                for e in range(2):
                    g_hi, g_lo = gate_hi[:, e * P:e * P + P], gate_lo[:, e * P:e * P + P]
                    h_hi, h_lo = hT_hi[:, bass.ds(b * S, S)], hT_lo[:, bass.ds(b * S, S)]
                    pe.matmul(bank[3][:, :], g_hi, h_hi, start=e == 0, stop=False)
                    pe.matmul(bank[3][:, :], g_lo, h_hi, start=False, stop=False)
                    mm = pe.matmul(bank[3][:, :], g_hi, h_lo, start=False, stop=e == 1)
                mm.then_inc(gate_done, 1)

            def turn_moe(b):
                pe.wait_ge(moe_done, b + 1)
                pe.wait_ge(y_done, b + 1)
                for t in range(TPB):
                    mm = pe.transpose(bank[4][:, t * P:t * P + P], moe_T[:, t * P:t * P + P], ident)
                mm.then_inc(moe_back, 1)

            def experts(b, par):
                more = not is_at(b, B - 1)
                gate(b)
                if is_at(b, 0):
                    attend(ITERS - 1, (ITERS - 1) % RING, 1)
                    out_product(ITERS - 2, odd=False)
                for c in range(CHUNKS + 2):
                    if c < CHUNKS:
                        up(b, c)
                    if c == 0 and is_at(b, 0):
                        turn_context(ITERS - 1)
                    if c == 2 and is_at(b, 0):
                        out_product(ITERS - 1, odd=True)
                    if c >= 2:
                        down(b, c - 2)
                    if c == 2 and not is_at(b, 0):
                        turn_moe(b - 1)
                    if c == 4 and more:
                        pe.wait_ge(back_in, b + 1)
                        pe.wait_ge(ln[1]["h32"], b + 1)
                        turn_back(b + 1, back_T)
                    if c == 9 and more:
                        turn_rows(b + 1)

            pe.wait_ge(w_lo_done, len(w_pieces))
            pe.wait_ge(ffn_ready, 1)
            pe.wait_ge(top_done, 8 * ITERS)
            batches(pe, experts)
            turn_moe(B - 1)


_INS = ['L0_attn_x', 'L0_attn_Wq', 'L0_attn_Wk', 'L0_attn_Wv', 'L0_attn_Wo', 'L0_attn_rel_emb', 'L0_ffn_gate_w',
        'L0_ffn_w1', 'L0_ffn_b1', 'L0_ffn_w2', 'L0_ffn_b2', 'L0_ffn_sw1', 'L0_ffn_sb1', 'L0_ffn_sw2', 'L0_ffn_sb2',
        'L0_c', 'L0_wmod']


def kernel(**inputs):
    import concourse.bacc as bacc
    from concourse.bass_utils import run_bass_kernel_spmd

    nc = bacc.Bacc("TRN2", target_bir_lowering=False, num_devices=1)
    arrays, ins, consts = {}, {}, {}
    for name in _INS:
        a = np.ascontiguousarray(inputs[name])
        arrays[f"in_{name}"] = a
        ins[name] = nc.dram_tensor(f"in_{name}", a.shape, mybir.dt.from_np(a.dtype), kind="ExternalInput").ap()
    for name, a in shape_constants().items():
        arrays[f"const_{name}"] = a
        consts[name] = nc.dram_tensor(f"const_{name}", a.shape, mybir.dt.from_np(a.dtype), kind="ExternalInput").ap()
    out = nc.dram_tensor("out_y", (B, S, D), F32, kind="ExternalOutput").ap()
    adaln_program(nc, ins, consts, out)
    r = run_bass_kernel_spmd(nc, [arrays], core_ids=[0])
    return r.results[0]["out_y"]
```
